# Optimizing a Trainium2 kernel written in Bass

```python
import numpy as np
import jax
import jax.numpy as jnp

def _softmax(x, axis=-1):
    return jax.nn.softmax(x, axis=axis)

def _gelu(x):
    return jax.nn.gelu(x, approximate=True)

def _silu(x):
    return jax.nn.silu(x)

def _sigmoid(x):
    return jax.nn.sigmoid(x)

def _layernorm(x, axis=-1, eps=1e-05):
    m = jnp.mean(x, axis=axis, keepdims=True)
    v = jnp.var(x, axis=axis, keepdims=True)
    return (x - m) / jnp.sqrt(v + eps)

def _scatter_add(tgt, idx, src, axis=0):
    return tgt.at[idx].add(src)

def _segment_sum(src, seg, n):
    return jax.ops.segment_sum(src, seg, n)
kernel_name = 'mk_gnn_preln_d2_gnn_r8_7b52c6'

def setup_inputs(seed: int=0):
    np.random.seed(seed)
    _w = jnp.asarray

    def _rec_inputs():
        import jax
        import jax.numpy as jnp
        _gk = jax.random.key(seed)
        x = -0.000202 + 1 * jax.random.normal(jax.random.fold_in(_gk, 1), (6250, 128), jnp.float32)
        src = jax.random.randint(jax.random.fold_in(_gk, 2), (100000,), 0, 6250, jnp.int32)
        dst = jnp.minimum((6250 * jax.random.uniform(jax.random.fold_in(_gk, 3), (100000,)) ** 2.0).astype(jnp.int32), 49999)
        _o = jnp.argsort(dst, stable=True)
        src = src[_o]
        dst = dst[_o]
        edge_attr_128 = -4.21973e-05 + 0.999841 * jax.random.normal(jax.random.fold_in(_gk, 11), (100000, 128), jnp.float32)
        return (x, src, dst, edge_attr_128)
    x, src, dst, edge_attr_128 = _rec_inputs()

    def _L0_gnn_setup():
        import jax, jax.numpy as jnp
        import numpy as np
        N = 6250
        E = 100000
        F_IN = 128
        H = 128

        def _sage_conv(x, src, dst, W_nbr, W_root, b):
            msgs = x[src]
            summed = jax.ops.segment_sum(msgs, dst, num_segments=N)
            deg = jax.ops.segment_sum(jnp.ones((src.shape[0], 1), x.dtype), dst, num_segments=N)
            agg = summed / jnp.maximum(deg, 1.0)
            return agg @ W_nbr + x @ W_root + b
        key = jax.random.key(seed)
        ks = jax.random.split(key, 8)
        s = 1.0 / np.sqrt(F_IN)
        sh = 1.0 / np.sqrt(H)
        return {'x': jax.random.normal(ks[0], (N, F_IN), dtype=jnp.float32), 'edge_index': jax.random.randint(ks[1], (2, E), 0, N, dtype=jnp.int64), 'W1_nbr': jax.random.normal(ks[2], (F_IN, H), dtype=jnp.float32) * s, 'W1_root': jax.random.normal(ks[3], (F_IN, H), dtype=jnp.float32) * s, 'b1': jnp.zeros((H,), dtype=jnp.float32), 'W2_nbr': jax.random.normal(ks[4], (H, H), dtype=jnp.float32) * sh, 'W2_root': jax.random.normal(ks[5], (H, H), dtype=jnp.float32) * sh, 'b2': jnp.zeros((H,), dtype=jnp.float32)}
    _L0_gnn_all = _L0_gnn_setup()
    _L0_gnn_in = {k: v for k, v in _L0_gnn_all.items() if k in ('W1_nbr', 'W1_root', 'b1', 'W2_nbr', 'W2_root', 'b2')}
    del _L0_gnn_all

    def _L1_gnn_setup():
        import jax, jax.numpy as jnp
        import numpy as np
        BN_EPS = 1e-05
        key = jax.random.key(seed)
        k1, k2, k3, k4 = jax.random.split(key, 4)
        N, E, H, ED = (12500, 75000, 128, 128)
        node_feats = jax.random.normal(k1, (N, H), dtype=jnp.float32)
        edge_feats = jax.random.normal(k2, (E, ED), dtype=jnp.float32)
        W = jax.random.normal(k3, (2 * H, 2 * H + ED), dtype=jnp.float32) * 0.05
        b = jnp.zeros((2 * H,), dtype=jnp.float32)
        gamma = jnp.ones((2 * H,), dtype=jnp.float32)
        beta = jnp.zeros((2 * H,), dtype=jnp.float32)
        edge_index = jax.random.randint(k4, (2, E), 0, N, dtype=jnp.int64)
        return {'node_feats': node_feats, 'edge_feats': edge_feats, 'W': W, 'b': b, 'gamma': gamma, 'beta': beta, 'edge_index': edge_index}
    _L1_gnn_all = _L1_gnn_setup()
    _L1_gnn_in = {k: v for k, v in _L1_gnn_all.items() if k in ('W', 'b', 'gamma', 'beta')}
    del _L1_gnn_all
    return {'x': x, 'src': src, 'dst': dst, 'edge_attr_128': edge_attr_128, 'L0_gnn_W1_nbr': _L0_gnn_in['W1_nbr'], 'L0_gnn_W1_root': _L0_gnn_in['W1_root'], 'L0_gnn_b1': _L0_gnn_in['b1'], 'L0_gnn_W2_nbr': _L0_gnn_in['W2_nbr'], 'L0_gnn_W2_root': _L0_gnn_in['W2_root'], 'L0_gnn_b2': _L0_gnn_in['b2'], 'L1_gnn_W': _L1_gnn_in['W'], 'L1_gnn_b': _L1_gnn_in['b'], 'L1_gnn_gamma': _L1_gnn_in['gamma'], 'L1_gnn_beta': _L1_gnn_in['beta']}

def reference(x, src, dst, edge_attr_128, L0_gnn_W1_nbr, L0_gnn_W1_root, L0_gnn_b1, L0_gnn_W2_nbr, L0_gnn_W2_root, L0_gnn_b2, L1_gnn_W, L1_gnn_b, L1_gnn_gamma, L1_gnn_beta):
    import jax
    import jax.numpy as jnp

    def _L0_gnn_ref(x, edge_index, W1_nbr, W1_root, b1, W2_nbr, W2_root, b2):
        import jax, jax.numpy as jnp
        import numpy as np
        N = 6250
        E = 100000
        F_IN = 128
        H = 128

        def _sage_conv(x, src, dst, W_nbr, W_root, b):
            msgs = x[src]
            summed = jax.ops.segment_sum(msgs, dst, num_segments=N)
            deg = jax.ops.segment_sum(jnp.ones((src.shape[0], 1), x.dtype), dst, num_segments=N)
            agg = summed / jnp.maximum(deg, 1.0)
            return agg @ W_nbr + x @ W_root + b
        src, dst = (edge_index[0], edge_index[1])
        h = jax.nn.relu(_sage_conv(x, src, dst, W1_nbr, W1_root, b1))
        out = _sage_conv(h, src, dst, W2_nbr, W2_root, b2)
        return out

    def _L1_gnn_ref(node_feats, edge_feats, W, b, gamma, beta, edge_index):
        import jax, jax.numpy as jnp
        import numpy as np
        BN_EPS = 1e-05
        H = node_feats.shape[1]
        src = edge_index[0]
        dst = edge_index[1]
        z = jnp.concatenate([node_feats[src], node_feats[dst], edge_feats], axis=1)
        z = z @ W.T + b
        mean = jnp.mean(z, axis=0)
        var = jnp.mean(jnp.square(z - mean), axis=0)
        z = (z - mean) * jax.lax.rsqrt(var + BN_EPS) * gamma + beta
        msg = jax.nn.sigmoid(z[:, :H]) * jax.nn.softplus(z[:, H:])
        agg = jnp.zeros_like(node_feats).at[src].add(msg)
        return node_feats + agg
    edge_index = jnp.stack([src, dst])
    h = jnp.maximum(_layernorm(x, axis=-1), 0.0)
    x = x + _L0_gnn_ref(h, edge_index, L0_gnn_W1_nbr, L0_gnn_W1_root, L0_gnn_b1, L0_gnn_W2_nbr, L0_gnn_W2_root, L0_gnn_b2)
    h = jnp.maximum(_layernorm(x, axis=-1), 0.0)
    x = x + _L1_gnn_ref(h, edge_attr_128, L1_gnn_W, L1_gnn_b, L1_gnn_gamma, L1_gnn_beta, edge_index)
    return x

_drawn_inputs = setup_inputs


def setup_inputs(seed=0):
    import zlib

    import numpy as np

    out = dict(_drawn_inputs(seed))
    spreads = {'L0_gnn_b1': (0.0, 0.316),
     'L0_gnn_b2': (0.0, 0.305),
     'L1_gnn_b': (0.0, 0.8),
     'L1_gnn_gamma': (1.0, 0.2),
     'L1_gnn_beta': (0.0, 0.1)}
    factors = {}
    for name, (base, spread) in spreads.items():
        noise = np.random.default_rng([zlib.crc32(name.encode()), seed]).standard_normal(out[name].shape)
        drawn = base * np.exp(spread * noise) if base else spread * noise
        out[name] = jnp.asarray(drawn.astype(out[name].dtype))
    for name, factor in factors.items():
        out[name] = (out[name] * factor).astype(out[name].dtype)
    return out
```

```python
import concourse.bass as bass
from concourse import mybir
from contextlib import ExitStack


def build_gnn(nc, x, src_cols, dst_cols, src_rows, dst_rows, edge_t, w1n, w1r, w2n, w2r, b1, b2,
              wab, wc, lb, gamma_beta, out, edges):
    F32, BF16, I32, I16 = mybir.dt.float32, mybir.dt.bfloat16, mybir.dt.int32, mybir.dt.int16
    ALU = mybir.AluOpType
    ACT = mybir.ActivationFunctionType
    AX = mybir.AxisListType
    ds = bass.ds

    P = 128
    NP, F = x.shape
    NT = NP // P
    NB = 7
    NI = NT // NB
    GT = 4
    GE = GT * P
    NG = edge_t.shape[0]
    TILES = NG * GT
    E = edges
    SL = 4
    ITER = NG // SL
    H2 = 2 * F
    EPS = 1e-5
    assert NI * NB == NT and ITER * SL == NG and NG % 4 == 0
    HALF = NG // 2

    ctx = ExitStack()
    with ctx:
        def sb(name, shape, dt=F32):
            return ctx.enter_context(nc.sbuf_tensor(name, shape, dt))

        def dram(name, shape, dt=F32):
            return nc.dram_tensor(name, shape, dt).ap()

        def sem(name):
            return ctx.enter_context(nc.semaphore(name))

        h_tab = [dram("h0_tab", (NP, F)), dram("h1_tab", (NP, F))]
        p_tab = dram("p_tab", (NP, H2))
        z_tab = dram("z_tab", (NG, P, 2 * GE))
        acc_tab = [dram(f"acc{k}_tab", (NP + P, F)) for k in range(GT)]
        win_tab = dram("win_tab", (NG,), I32)
        src16_tab = dram("src16_tab", (NG, GE), I16)
        dst16_tab = dram("dst16_tab", (NG, GE), I16)

        X = sb("X", [P, NT, F])
        H = sb("H", [P, NT, F])
        Q = sb("Q", [P, 3, NT, H2], BF16)
        stats = sb("stats", [P, 2, NG, 6])
        src_i = sb("src_i", [P, TILES], I32)
        src_f = sb("src_f", [P, TILES])
        dst_f = sb("dst_f", [P, TILES])
        scat_i = sb("scat_i", [P, TILES], I32)
        W1N, W1R, W2N, W2R = (sb(n, [P, F]) for n in ("W1N", "W1R", "W2N", "W2R"))
        WAB = sb("WAB", [P, 2 * H2])
        WC = sb("WC", [P, H2])
        B1, B2 = sb("B1", [P, F]), sb("B2", [P, F])
        LB = sb("LB", [P, H2])
        GB = sb("GB", [P, 4])
        iota_i = sb("iota_i", [P, F], I32)
        iota = sb("iota", [P, F])
        lower = sb("lower", [P, F])
        ident = sb("ident", [P, F])
        win_i = sb("win_i", [P, 2, NT], I32)
        wneg = sb("wneg", [P, NT])
        wpos = sb("wpos", [P, NT])
        words = sb("words", [1, NG], I32)
        idx_slot = sb("idx_slot", [P, SL * GT], I32)
        small = sb("small", [P, 8, NB])
        bn = sb("bn", [P, 24])
        ARENA = 13000
        arena = sb("arena", [P, ARENA])

        def carve(at, *shape, dt=F32):
            n = 1
            for d in shape:
                n *= d
            w = n if dt in (F32, I32) else n // 2
            assert at + w <= ARENA, (at, w)
            v = arena[:, at:at + w]
            if dt != F32:
                v = v.bitcast(dt)
            if len(shape) == 2:
                v = v.rearrange("p (a b) -> p a b", a=shape[0])
            elif len(shape) == 3:
                v = v.rearrange("p (a b c) -> p a b c", a=shape[0], b=shape[1])
            return v, at + w

        AGG, a_agg = carve(0, NT, F + 1)
        rows, a = carve(a_agg, SL * GT, F + 1)
        onehot, a = carve(a, GT, P)
        s16, a = carve(a, 2, GE, dt=I16)
        junk, a = carve(a, P)
        cnt, a = carve(a, TILES)
        dr_i, b = carve(0, 2, GE, dt=I32)
        sr_i, b = carve(b, 2, GE, dt=I32)
        dr16, b = carve(b, 2, GE, dt=I16)
        sr16, b = carve(b, 2, GE, dt=I16)
        dst_i, b = carve(b, TILES, dt=I32)
        gmin, b = carve(b, 2)
        gmax, b = carve(b, 2)
        gmn_i, b = carve(b, 2, dt=I32)
        gmx_i, b = carve(b, 2, dt=I32)
        gw_i, b = carve(b, 2, dt=I32)
        assert b <= a_agg
        zero, _ = carve(a_agg, 10 * F)
        mean_s, a = carve(a_agg, NB, F)
        h_s, a = carve(a, NB, F)
        mean_t, a = carve(a, NB, F)
        h_t, a = carve(a, NB, F)
        o_s, a = carve(a, NB, F)
        xc, a = carve(a, NB, F)
        hq_s, a = carve(0, NB, F)
        hq_t, a = carve(a, NB, F)
        p_s, a = carve(a, NB, H2)
        q_s, a = carve(a, NB, H2)
        prow, a = carve(0, SL * GT, H2)
        ebuf, a = carve(a, 2, GE)
        d16, a = carve(a, 2, GE, dt=I16)
        oht, a = carve(a, GE, dt=BF16)
        zt, a = carve(a, 2, 2 * GE)
        zb, a = carve(a, 2, 2 * GE)
        zin, a = carve(0, 2, 2 * GE)
        s16b, a = carve(a, 2, GE, dt=I16)
        U, a = carve(a, 2, GE)
        R, a = carve(a, 2, GE)
        L, a = carve(a, 2, GE)
        msg_t, a = carve(a, 2, GE)
        msg, a = carve(a, 2, GE)
        same, a = carve(a, 2, GE)
        drow, a = carve(a, SL, GE)
        fin, a = carve(0, 2, GT, NB * F)

        PS = ctx.enter_context(nc.psum_tensor("PS", [P, 8, 512], F32))
        ps_agg = PS[:, 0, 0:F + 1]

        def banks(n):
            return PS[:, n:n + 2, :].rearrange("p a b -> p (a b)")[:, 0:NB * F]

        def wide(n):
            return PS[:, n:n + 4, :].rearrange("p a b -> p (a b)")[:, 0:NB * H2]

        def bc(ap, n):
            return ap.unsqueeze(2).to_broadcast([ap.shape[0], ap.shape[1], n])

        def rep(ap, n):
            return ap.unsqueeze(1).to_broadcast([ap.shape[0], n, ap.shape[1]])

        class Sems:
            pass

        def ring(name, n):
            return [sem(f"{name}{k}") for k in range(n)]

        in_idx, in_x, in_w = sem("in_idx"), sem("in_x"), sem("in_w")
        iota_done, consts = sem("iota_done"), sem("consts")
        natural_ready = sem("natural_ready")
        natural_stored, words_in = sem("natural_stored"), sem("words_in")
        zero_ready, acc_zeroed = sem("zero_ready"), sem("acc_zeroed")
        wait_done = sem("wait_done")
        chain = sem("dve_chain")
        ln = Sems()
        ln.step, ln.var, ln.root = sem("ln_step"), sem("ln_var"), sem("ln_root")
        ln.ready, ln.stored = sem("ln_ready"), sem("ln_stored")
        conv, node = [], []
        for c in range(2):
            k = Sems()
            k.onehot_ready, k.sum_ready, k.sum_added = sem(f"conv{c}_onehot_ready"), sem(f"conv{c}_sum_ready"), sem(f"conv{c}_sum_added")
            k.group_done, k.finished = sem(f"conv{c}_group_done"), sem(f"conv{c}_finished")
            k.idx_ready, k.rows_landed = ring(f"conv{c}_idx_ready", SL), ring(f"conv{c}_rows_landed", SL)
            conv.append(k)
            n = Sems()
            n.step, n.mean_ready, n.h_staged = sem(f"node{c}_step"), sem(f"node{c}_mean_ready"), sem(f"node{c}_h_staged")
            n.turned, n.mean_t_ready, n.h_t_ready = sem(f"node{c}_turned"), sem(f"node{c}_mean_t_ready"), sem(f"node{c}_h_t_ready")
            n.product, n.var, n.root = sem(f"node{c}_product"), sem(f"node{c}_var"), sem(f"node{c}_root")
            n.ready, n.stored = sem(f"node{c}_ready"), sem(f"node{c}_stored")
            node.append(n)
        s16_landed, counted = ring("s16_landed", 2), sem("counted")
        pq = Sems()
        pq.staged, pq.turned, pq.evicted = sem("pq_staged"), sem("pq_turned"), sem("pq_evicted")
        pq.product, pq.rest, pq.part = sem("pq_product"), sem("pq_rest"), sem("pq_part")
        pq.p_ready, pq.p_stored = sem("pq_p_ready"), sem("pq_p_stored")
        p1 = Sems()
        p1.oht_ready, p1.oht_used, p1.evicted = sem("pass1_oht_ready"), sem("pass1_oht_used"), sem("pass1_evicted")
        p1.done, p1.z_ready, p1.z_free = sem("pass1_done"), sem("pass1_z_ready"), sem("pass1_z_free")
        p1.stats_done = sem("pass1_stats_done")
        p1.idx_ready, p1.rows_landed = ring("pass1_idx_ready", SL), ring("pass1_rows_landed", SL)
        p1.edges_landed, p1.z_stored = ring("pass1_edges_landed", 2), ring("pass1_z_stored", 2)
        norm = Sems()
        norm.step, norm.var, norm.root = sem("norm_step"), sem("norm_var"), sem("norm_root")
        norm.ready = sem("norm_ready")
        p2 = Sems()
        p2.act_step, p2.dve_step, p2.funcs_done = sem("pass2_act_step"), sem("pass2_dve_step"), sem("pass2_funcs_done")
        p2.same_ready, p2.msg_t_ready, p2.turned = sem("pass2_same_ready"), sem("pass2_msg_t_ready"), sem("pass2_turned")
        p2.msg_ready, p2.merged, p2.drow_ready = sem("pass2_msg_ready"), sem("pass2_merged"), sem("pass2_drow_ready")
        p2.z_in, p2.scattered = ring("pass2_z_in", 2), ring("pass2_scattered", GT)
        fin_in, fin_out, fin_step = ring("fin_in", 2), ring("fin_out", 2), sem("fin_step")

        def stepper(eng, s, base=0):
            n = [0]

            def step(ins):
                n[0] += 1
                ins.then_inc(s, 1)
                eng.wait_ge(s, base + n[0])
            step.n = n
            return step

        def windows(eng, g):
            word = nc.values_load(words[0:1, ds(g, 1)], engines=(eng.engine,), min_val=0,
                                  max_val=64 * (NT - 1) + NT - 1,
                                  skip_runtime_bounds_check_because="dst lies in the padded nodes")
            return eng.snap(word // 64), eng.snap(word % 64 + 1)

        def window(w):
            return nc.s_assert_within(w, 0, NT - 1,
                                      skip_runtime_bounds_check_because="dst lies in the padded nodes")

        def tick(eng, reg):
            eng.reg_add(reg, reg, 1)
            return eng.snap(reg, min_val=1, max_val=NG * NT)

        def rows_of(tab, i):
            return tab[ds(i * (NB * P), NB * P), :].rearrange("(j p) f -> p j f", p=P)

        def row16(tab, g):
            return tab[ds(g, 1), :].to_broadcast([P, GE])

        def square(tab, g):
            return tab[ds(g, 1)].rearrange("a p e -> (a p) e")

        block = ctx.enter_context(nc.Block())

        @block.sync
        def _(sp):
            sp.dma_start(dr_i[0:HALF], dst_rows.rearrange("(p c) e -> p c e", c=2)).then_inc(in_idx, 16)
            sp.dma_start(sr_i[0:HALF], src_rows.rearrange("(p c) e -> p c e", c=2)).then_inc(in_idx, 16)
            sp.dma_start(dst_i, dst_cols).then_inc(in_idx, 16)
            sp.dma_start(src_i[:], src_cols).then_inc(in_idx, 16)
            sp.dma_start(X[:], x.rearrange("(j p) f -> p j f", p=P)).then_inc(in_x, 16)
            for t, d in ((W1N, w1n), (W1R, w1r), (W2N, w2n), (W2R, w2r), (WC, wc), (WAB, wab),
                         (B1, b1.to_broadcast([P, F])), (B2, b2.to_broadcast([P, F])),
                         (LB, lb.to_broadcast([P, H2])), (GB, gamma_beta)):
                sp.dma_start(t[:], d).then_inc(in_w, 16)
            sp.wait_ge(natural_ready, 3)
            sp.dma_start(dst16_tab.rearrange("(p c) e -> p c e", c=2), dr16[0:HALF]).then_inc(natural_stored, 16)
            sp.dma_start(src16_tab.rearrange("(p c) e -> p c e", c=2), sr16[0:HALF]).then_inc(natural_stored, 16)
            sp.dma_start(win_tab.rearrange("(p c) -> p c", c=2), gw_i[0:HALF]).then_inc(natural_stored, 16)
            sp.wait_ge(natural_stored, 48)
            sp.dma_start(words[:], win_tab.rearrange("(a g) -> a g", a=1)).then_inc(words_in, 16)
            sp.wait_ge(zero_ready, 1)
            for k in range(1, GT):
                sp.dma_start(acc_tab[k].rearrange("(p r c) f -> p r (c f)", p=P, c=10),
                             rep(zero, 5)).then_inc(acc_zeroed, 16)
            sp.dma_start(acc_tab[0][NP:NP + P, :], zero[:, 0:F]).then_inc(acc_zeroed, 16)
            with sp.Fori(0, NI) as i:
                sp.wait_ge(ln.ready, i + 1)
                sp.dma_start(rows_of(h_tab[0], i), H[:, ds(i * NB, NB), :]).then_inc(ln.stored, 16)
            with sp.Fori(0, NG // 2) as i:
                for q in range(2):
                    sp.wait_ge(counted, i * (2 * GT) + (q + 1) * GT)
                    sp.dma_start(s16[:, q, :], row16(src16_tab, i * 2 + q)).then_inc(s16_landed[q], 16)
            for c, tab, src in ((0, h_tab[1], H), (1, acc_tab[0], X)):
                with sp.Fori(0, NI) as i:
                    sp.wait_ge(node[c].ready, i + 1)
                    sp.dma_start(rows_of(tab, i), src[:, ds(i * NB, NB), :]).then_inc(node[c].stored, 16)
            with sp.Fori(0, NI) as i:
                sp.wait_ge(pq.p_ready, i + 1)
                sp.dma_start(rows_of(p_tab, i), p_s).then_inc(pq.p_stored, 16)

            def load_edges(g, q):
                sp.dma_start(ebuf[:, q, :], square(edge_t, g)).then_inc(p1.edges_landed[q], 16)
                sp.dma_start(d16[:, q, :], row16(dst16_tab, g)).then_inc(p1.edges_landed[q], 16)

            def store_z(g, q):
                sp.wait_ge(p1.z_ready, g + 3)
                sp.dma_start(square(z_tab, g), zb[:, q, :]).then_inc(p1.z_stored[q], 16)

            sp.wait_ge(pq.p_stored, 16 * NI)
            sp.wait_ge(pq.part, 3 * NI)
            sp.sem_inc(p1.z_free, 2)
            load_edges(0, 0)
            load_edges(1, 1)
            for g in range(2):
                store_z(g, g)
                sp.wait_ge(p1.done, g + SL + 1)
                load_edges(g + 2, g)
            with sp.Fori(1, NG // 2 - 1) as i:
                for q in range(2):
                    g = i * 2 + q
                    sp.wait_ge(p1.z_stored[q], i * 16)
                    sp.sem_inc(p1.z_free, 1)
                    store_z(g, q)
                    sp.wait_ge(p1.done, g + SL + 1)
                    load_edges(g + 2, q)
            for q in range(2):
                sp.wait_ge(p1.z_stored[q], 16 * (NG // 2 - 1))
                sp.sem_inc(p1.z_free, 1)
                store_z(NG - 2 + q, q)
            for q in range(2):
                sp.wait_ge(p1.z_stored[q], 16 * (NG // 2))

            sp.wait_ge(norm.ready, 1)
            with sp.Fori(0, NG // 2) as i:
                for q in range(2):
                    g = i * 2 + q
                    sp.wait_ge(p2.funcs_done, g + 1)
                    sp.wait_ge(p2.same_ready, g + 1)
                    sp.dma_start(zin[:, q, :], square(z_tab, g)).then_inc(p2.z_in[q], 16)
                    sp.dma_start(s16b[:, q, :], row16(src16_tab, g)).then_inc(p2.z_in[q], 16)

            def store_out(i):
                q = i % 2
                sp.wait_ge(fin_step, 3 * (i + 1))
                sp.dma_start(rows_of(out, i), fin[:, q, 0, :].rearrange("p (j f) -> p j f", f=F)
                             ).then_inc(fin_out[q], 16)
            for k in range(GT):
                sp.wait_ge(p2.scattered[k], 16 * NG)
            for i in range(NI):
                q = i % 2
                if i >= 2:
                    sp.wait_ge(fin_out[q], 16 * (i // 2))
                for k in range(GT):
                    sp.dma_start(fin[:, q, k, :].rearrange("p (j f) -> p j f", f=F),
                                 rows_of(acc_tab[k], i)).then_inc(fin_in[q], 16)
                if i >= 1:
                    store_out(i - 1)
            store_out(NI - 1)
            sp.wait_ge(fin_out[0], 16 * ((NI + 1) // 2))
            sp.wait_ge(fin_out[1], 16 * (NI // 2))

        @block.gpsimd
        def _(pool):
            nc.gpsimd.iota(iota_i[:], pattern=[[1, F]], base=0, channel_multiplier=0).then_inc(iota_done, 1)
            nc.gpsimd.iota(win_i[:, 0, :], pattern=[[-P, NT]], base=0, channel_multiplier=0).then_inc(iota_done, 1)
            nc.gpsimd.iota(win_i[:, 1, :], pattern=[[P, NT]], base=0, channel_multiplier=1).then_inc(iota_done, 1)

            def gather_all(k, table, buf, width):
                with pool.Fori(0, ITER) as i:
                    for s in range(SL):
                        pool.wait_ge(k.idx_ready[s], i + 1)
                        pool.sem_inc(wait_done, 1)
                        for t in range(s * GT, s * GT + GT):
                            nc.gpsimd.indirect_dma_start(buf[:, t, 0:width], None, table,
                                                         bass.IndirectOffsetOnAxis(idx_slot[:, t:t + 1], 0)
                                                         ).then_inc(k.rows_landed[s], 16)

            pool.wait_ge(ln.stored, 16 * NI)
            gather_all(conv[0], h_tab[0], rows, F)
            pool.wait_ge(node[0].stored, 16 * NI)
            gather_all(conv[1], h_tab[1], rows, F)
            pool.wait_ge(pq.p_stored, 16 * NI)
            gather_all(p1, p_tab, prow, H2)

            def scatter(g, s, first=False):
                pool.wait_ge(p2.drow_ready, g + 3)
                for k in range(GT):
                    if not first:
                        pool.wait_ge(p2.scattered[k], g * 16)
                    pool.sem_inc(wait_done, 1)
                    t = s * GT + k
                    nc.gpsimd.indirect_dma_start(acc_tab[k], bass.IndirectOffsetOnAxis(idx_slot[:, t:t + 1], 0),
                                                 drow[:, s, k * F:(k + 1) * F], None,
                                                 compute_op=ALU.add).then_inc(p2.scattered[k], 16)
            pool.wait_ge(acc_zeroed, 16 * GT)
            pool.wait_ge(node[1].stored, 16 * NI)
            for s in range(SL):
                scatter(s, s, first=s == 0)
            with pool.Fori(1, ITER) as i:
                for s in range(SL):
                    scatter(i * SL + s, s)

        @block.scalar
        def _(act):
            act.wait_ge(in_idx, 64)

            def put_idx(table, g, s, signal):
                return nc.scalar.copy(idx_slot[:, s * GT:(s + 1) * GT], table[:, ds(g * GT, GT)]).then_inc(signal, 1)

            with act.Fori(0, NI) as i:
                act.wait_ge(ln.var, i + 1)
                nc.scalar.activation(small[:, 3, :], small[:, 2, :], ACT.Sqrt).then_inc(ln.root, 1)

            for c in range(2):
                k, n = conv[c], node[c]
                for s in range(SL):
                    put_idx(src_i, s, s, k.idx_ready[s])
                with act.Fori(0, ITER - 1) as i:
                    for s in range(SL):
                        g = i * SL + s
                        act.wait_ge(k.group_done, g + 1)
                        put_idx(src_i, g + SL, s, k.idx_ready[s])
                act.wait_ge(k.group_done, NG)
                act.wait_ge(k.finished, 1)
                with act.Fori(0, NI) as i:
                    nc.scalar.copy(h_s, H[:, ds(i * NB, NB), :]).then_inc(n.h_staged, 1)
                    act.wait_ge(n.turned, i + 1)
                    nc.scalar.copy(h_t.rearrange("p a b -> p (a b)"), banks(2)).then_inc(n.h_t_ready, 1)
                    if c == 1:
                        act.wait_ge(n.var, i + 1)
                        nc.scalar.activation(small[:, 3, :], small[:, 2, :], ACT.Sqrt).then_inc(n.root, 1)

            act.wait_ge(node[1].ready, NI)
            def pq_group(i, first=False):
                nc.scalar.copy(hq_s, H[:, ds(i * NB, NB), :]).then_inc(pq.staged, 1)
                act.wait_ge(pq.product, i + 1)
                if not first:
                    act.wait_ge(pq.p_stored, i * 16)
                nc.scalar.copy(p_s.rearrange("p a b -> p (a b)"), wide(0)).then_inc(pq.p_ready, 1)
                for j in range(3):
                    act.wait_ge(pq.rest, i * 3 + j + 1)
                    nc.scalar.copy(Q[:, j, ds(i * NB, NB), :], q_s).then_inc(pq.part, 1)
            pq_group(0, first=True)
            with act.Fori(1, NI) as i:
                pq_group(i)

            def evict(g, q):
                act.wait_ge(p1.done, g + SL + 1)
                act.wait_ge(p1.z_ready, g + 1)
                nc.scalar.copy(zt[:, q, :], PS[:, 2 * q:2 * q + 2, :].rearrange("p a b -> p (a b)")
                               ).then_inc(p1.evicted, 1)
            act.wait_ge(pq.p_stored, 16 * NI)
            act.sem_inc(p1.evicted, 2)
            for s in range(SL):
                put_idx(src_i, s, s, p1.idx_ready[s])
            with act.Fori(0, ITER - 1) as i:
                for s in range(SL):
                    g = i * SL + s
                    evict(g, s % 2)
                    put_idx(src_i, g + SL, s, p1.idx_ready[s])
            for s in range(SL):
                evict(NG - SL + s, s % 2)

            act.wait_ge(norm.var, 1)
            nc.scalar.activation(bn[:, 6:8], bn[:, 4:6], ACT.Sqrt).then_inc(norm.root, 1)

            def funcs(g, q, n):
                act.wait_ge(p2.z_in[q], n * 32 + 32)
                act.wait_ge(p2.msg_t_ready, g + 1)
                za, zc = zin[:, q, 0:GE], zin[:, q, GE:2 * GE]
                nc.scalar.activation(U[:, q, :], za, ACT.Exp, scale=bn[:, 12:13], bias=bn[:, 13:14]
                                     ).then_inc(p2.act_step, 1)
                nc.scalar.activation(L[:, q, :], zc, ACT.Abs, scale=bn[:, 9:10], bias=bn[:, 11:12]
                                     ).then_inc(p2.act_step, 1)
                nc.scalar.activation(R[:, q, :], zc, ACT.Relu, scale=bn[:, 9:10], bias=bn[:, 11:12]
                                     ).then_inc(p2.act_step, 1)
                act.wait_ge(p2.act_step, g * 4 + 2)
                nc.scalar.activation(L[:, q, :], L[:, q, :], ACT.Exp, scale=-1.0).then_inc(p2.act_step, 1)
                act.wait_ge(p2.act_step, g * 4 + 4)
                nc.scalar.activation(L[:, q, :], L[:, q, :], ACT.Ln, bias=1.0).then_inc(p2.funcs_done, 1)

            def drain_rows(g, s, first=False):
                act.wait_ge(p2.merged, g + 3)
                if not first:
                    for k in range(GT):
                        act.wait_ge(p2.scattered[k], g * 16 - 16 * (SL - 1))
                nc.scalar.copy(drow[:, s, :], PS[:, 4 + s % 2, :])
                put_idx(scat_i, g, s, p2.drow_ready)

            act.wait_ge(norm.ready, 1)
            act.sem_inc(p2.funcs_done, 2)
            act.sem_inc(p2.drow_ready, 2)
            for g in range(SL):
                funcs(g, g % 2, g // 2)
                if g >= 2:
                    drain_rows(g - 2, g - 2, first=True)
            for g in range(SL, 2 * SL):
                funcs(g, g % 2, g // 2)
                drain_rows(g - 2, (g - 2) % SL, first=g - 2 < SL)
            with act.Fori(2, ITER) as i:
                for s in range(SL):
                    g = i * SL + s
                    funcs(g, s % 2, i * 2 + s // 2)
                    drain_rows(g - 2, (s - 2) % SL)
            for g in (NG - 2, NG - 1):
                drain_rows(g, g % SL)

        @block.vector
        def _(dve):
            v = nc.vector
            step = stepper(dve, chain)
            dve.wait_ge(iota_done, 3)
            step(v.tensor_copy(iota[:], iota_i[:]))
            step(v.tensor_copy(wneg[:], win_i[:, 0, :]))
            step(v.tensor_copy(wpos[:], win_i[:, 1, :]))
            step(v.tensor_scalar(ident[:], iota[:], wpos[:, 0:1], None, ALU.is_equal))
            v.tensor_scalar(lower[:], iota[:], wpos[:, 0:1], None, ALU.is_lt).then_inc(consts, 1)
            v.memset(zero, 0.0).then_inc(zero_ready, 1)
            dve.wait_ge(in_idx, 64)
            d, s_ = dr_i[0:HALF], sr_i[0:HALF]
            v.tensor_copy(dr16[0:HALF], d).then_inc(natural_ready, 1)
            v.tensor_copy(sr16[0:HALF], s_).then_inc(natural_ready, 1)
            step(v.tensor_reduce(gmn_i[0:HALF], d, AX.X, ALU.min))
            step(v.tensor_reduce(gmx_i[0:HALF], d, AX.X, ALU.max))
            step(v.tensor_scalar(gmn_i[0:HALF], gmn_i[0:HALF], 7, None, ALU.logical_shift_right))
            step(v.tensor_scalar(gmx_i[0:HALF], gmx_i[0:HALF], 7, None, ALU.logical_shift_right))
            v.scalar_tensor_tensor(gw_i[0:HALF], gmn_i[0:HALF], 64.0, gmx_i[0:HALF], ALU.mult, ALU.add
                                   ).then_inc(natural_ready, 1)
            step(v.tensor_copy(src_f[:], src_i[:]))
            step(v.tensor_copy(dst_f[:], dst_i))

            def inverse_root(step, var, root, inv, tmp):
                step(v.reciprocal(inv, root))
                step(v.tensor_tensor(tmp, inv, inv, ALU.mult))
                step(v.tensor_tensor(tmp, tmp, var, ALU.mult))
                step(v.tensor_scalar(tmp, tmp, -0.5, 1.5, ALU.mult, ALU.add))
                step(v.tensor_tensor(inv, inv, tmp, ALU.mult))

            def layer_norm(i, step, var_ready, root, out_h):
                xs = X[:, ds(i * NB, NB), :]
                dve.sem_inc(wait_done, 1)
                step(v.tensor_reduce(small[:, 0, :], xs, AX.X, ALU.add))
                step(v.tensor_scalar(small[:, 1, :], small[:, 0, :], -1.0 / F, None, ALU.mult))
                step(v.tensor_tensor(xc, xs, bc(small[:, 1, :], F), ALU.add))
                step(v.tensor_tensor(o_s, xc, xc, ALU.mult))
                step(v.tensor_reduce(small[:, 0, :], o_s, AX.X, ALU.add))
                v.tensor_scalar(small[:, 2, :], small[:, 0, :], 1.0 / F, EPS, ALU.mult, ALU.add
                                ).then_inc(var_ready, 1)
                dve.wait_ge(root, i + 1)
                inverse_root(step, small[:, 2, :], small[:, 3, :], small[:, 4, :], small[:, 5, :])
                return v.scalar_tensor_tensor(out_h, xc, 0.0, bc(small[:, 4, :], F), ALU.max, ALU.mult)

            dve.wait_ge(in_x, 16)
            dve.wait_ge(acc_zeroed, 16 * GT)
            LN_STEPS = 10
            with dve.Fori(0, NI) as i:
                st = stepper(dve, ln.step, i * LN_STEPS)
                layer_norm(i, st, ln.var, ln.root, H[:, ds(i * NB, NB), :]).then_inc(ln.ready, 1)
                dve.wait_ge(ln.ready, i + 1)
                assert st.n[0] == LN_STEPS

            def sum_by_window(k, g, pair):
                lo, hi = windows(dve, g)
                with dve.Fori(lo, hi) as w:
                    n, w = tick(dve, pair), window(w)
                    v.scalar_tensor_tensor(onehot, bc(dst_f[:, ds(g * GT, GT)], P), wneg[:, ds(w, 1)],
                                           rep(iota[:], GT), ALU.add, ALU.is_equal).then_inc(k.onehot_ready, 1)
                    dve.wait_ge(k.sum_ready, n)
                    dve.wait_ge(k.sum_added, n)
                    a = AGG[:, ds(w, 1), :].rearrange("p a b -> p (a b)")
                    v.tensor_tensor(a, a, ps_agg, ALU.add).then_inc(k.sum_added, 1)

            def count_repeats(g, q, n):
                dve.wait_ge(s16_landed[q], n * 16 + 16)
                for k in range(GT):
                    dve.wait_ge(counted, g * GT + 2 * GT + k)
                    v.scalar_tensor_tensor(junk, s16[:, q, k * P:(k + 1) * P], src_f[:, ds(g * GT + k, 1)],
                                           lower[:], ALU.is_equal, ALU.mult,
                                           accum_out=cnt[:, ds(g * GT + k, 1)]).then_inc(counted, 1)

            dve.wait_ge(natural_stored, 48)
            dve.wait_ge(words_in, 16)
            NODE_STEPS = [3, 15]
            for c in range(2):
                k, n = conv[c], node[c]
                v.memset(AGG, 0.0).then_inc(k.sum_added, 1)
                step(v.memset(rows[:, :, F:F + 1], 1.0))
                pair = dve.alloc_register(f"dve_pair{c}")
                dve.reg_mov(pair, 0)
                if c == 0:
                    dve.sem_inc(counted, 2 * GT)
                with dve.Fori(0, NG // 2) as i:
                    for q in range(2):
                        sum_by_window(k, i * 2 + q, pair)
                        if c == 0:
                            count_repeats(i * 2 + q, q, i)
                dve.wait_ge(k.group_done, NG)
                dve.wait_ge(k.sum_added, tick(dve, pair))
                if c == 0:
                    dve.wait_ge(counted, (NG + 2) * GT)
                    big, _ = carve(a_agg, TILES)
                    step(v.tensor_scalar(bn[:, 0:1], wpos[:, 0:1], float(NP), None, ALU.add))
                    step(v.tensor_scalar(big, src_f[:], -1.0, bn[:, 0:1], ALU.mult, ALU.add))
                    step(v.tensor_scalar(cnt, cnt, 0.0, None, ALU.is_gt))
                    step(v.tensor_tensor(big, big, cnt, ALU.mult))
                    step(v.tensor_tensor(scat_i[:], big, src_f[:], ALU.add))
                dve.sem_inc(k.finished, 1)
                with dve.Fori(0, NI) as i:
                    st = stepper(dve, n.step, i * NODE_STEPS[c])
                    deg = AGG[:, ds(i * NB, NB), F:F + 1].rearrange("p a b -> p (a b)")
                    st(v.tensor_scalar(small[:, 6, :], deg, 1.0, None, ALU.max))
                    st(v.reciprocal(small[:, 7, :], small[:, 6, :]))
                    v.tensor_tensor(mean_s, AGG[:, ds(i * NB, NB), 0:F], bc(small[:, 7, :], F), ALU.mult
                                    ).then_inc(n.mean_ready, 1)
                    dve.wait_ge(n.turned, i + 1)
                    v.tensor_copy(mean_t.rearrange("p a b -> p (a b)"), banks(0)).then_inc(n.mean_t_ready, 1)
                    dve.wait_ge(n.product, i + 1)
                    hs, xs = H[:, ds(i * NB, NB), :], X[:, ds(i * NB, NB), :]
                    product = banks(4).rearrange("p (a b) -> p a b", b=F)
                    st(v.tensor_tensor(o_s, product, rep((B1 if c == 0 else B2)[:], NB), ALU.add))
                    if c == 0:
                        v.tensor_scalar(hs, o_s, 0.0, None, ALU.max).then_inc(n.ready, 1)
                    else:
                        st(v.tensor_tensor(xs, xs, o_s, ALU.add))
                        st(layer_norm(i, st, n.var, n.root, hs))
                        v.tensor_tensor(xs, xs, hs, ALU.add).then_inc(n.ready, 1)
                    dve.wait_ge(n.ready, i + 1)
                    assert st.n[0] == NODE_STEPS[c], st.n

            with dve.Fori(0, NI) as i:
                dve.wait_ge(pq.turned, i + 1)
                v.tensor_copy(hq_t.rearrange("p a b -> p (a b)"), banks(0)).then_inc(pq.evicted, 1)
                dve.wait_ge(pq.product, i + 1)
                v.tensor_tensor(q_s, wide(4).rearrange("p (a b) -> p a b", b=H2), rep(LB[:], NB), ALU.add
                                ).then_inc(pq.rest, 1)
                for j in range(2):
                    dve.wait_ge(pq.part, i * 3 + j + 1)
                    v.tensor_tensor(q_s, q_s, Q[:, j, ds(i * NB, NB), :], ALU.subtract).then_inc(pq.rest, 1)
                dve.wait_ge(pq.part, i * 3 + 3)

            def onehot_by_window(g, q, n, pair):
                lo, hi = windows(dve, g)
                dve.wait_ge(p1.edges_landed[q], n * 32 + 32)
                with dve.Fori(lo, hi) as w:
                    m, w = tick(dve, pair), window(w)
                    dve.wait_ge(p1.oht_used, m)
                    v.tensor_scalar(oht, d16[:, q, :], wpos[:, ds(w, 1)], None, ALU.is_equal
                                    ).then_inc(p1.oht_ready, 1)

            def finish_z(g, q, valid=GE):
                dve.wait_ge(p1.evicted, g + 3)
                dve.wait_ge(p1.z_free, g + 1)
                dve.wait_ge(p1.stats_done, g + 1)
                v.tensor_tensor(zb[:, q, :], zt[:, q, :], PS[:, 4 + 2 * q:6 + 2 * q, :].rearrange("p a b -> p (a b)"),
                                ALU.add).then_inc(p1.z_ready, 1)
                dve.wait_ge(p1.z_ready, g + 3)
                for h in range(2):
                    ins = v.bn_stats(stats[:, h, ds(g, 1), :].rearrange("p a b -> p (a b)"),
                                     zb[:, q, h * GE:h * GE + valid])
                ins.then_inc(p1.stats_done, 1)

            dve.wait_ge(pq.p_stored, 16 * NI)
            dve.sem_inc(p1.z_ready, 2)
            dve.sem_inc(p1.stats_done, 2)
            pair = dve.alloc_register("dve_pair2")
            dve.reg_mov(pair, 0)
            onehot_by_window(0, 0, 0, pair)
            with dve.Fori(0, NG // 2 - 1) as i:
                onehot_by_window(i * 2 + 1, 1, i, pair)
                finish_z(i * 2, 0)
                onehot_by_window(i * 2 + 2, 0, i + 1, pair)
                finish_z(i * 2 + 1, 1)
            onehot_by_window(NG - 1, 1, NG // 2 - 1, pair)
            finish_z(NG - 2, 0)
            finish_z(NG - 1, 1, valid=E - (NG - 1) * GE)
            dve.wait_ge(p1.stats_done, NG + 2)

            nst = stepper(dve, norm.step)
            for h in range(2):
                nst(v.bn_aggr(bn[:, 2 * h:2 * h + 2], stats[:, h].rearrange("p a b -> p (a b)")))
            mv = bn[:, 0:4].rearrange("p (h k) -> p k h", k=2)
            v.tensor_scalar(bn[:, 4:6], mv[:, 1, :], EPS, None, ALU.add).then_inc(norm.var, 1)
            dve.wait_ge(norm.root, 1)
            inverse_root(nst, bn[:, 4:6], bn[:, 6:8], bn[:, 14:16], bn[:, 16:18])
            nst(v.tensor_tensor(bn[:, 8:10], bn[:, 14:16], GB[:, 0:2], ALU.mult))
            nst(v.tensor_tensor(bn[:, 18:20], mv[:, 0, :], bn[:, 8:10], ALU.mult))
            nst(v.tensor_tensor(bn[:, 10:12], GB[:, 2:4], bn[:, 18:20], ALU.subtract))
            nst(v.tensor_scalar(bn[:, 12:13], bn[:, 8:9], -1.0, None, ALU.mult))
            v.tensor_scalar(bn[:, 13:14], bn[:, 10:11], -1.0, None, ALU.mult).then_inc(norm.ready, 1)

            def messages(g, q, n):
                dve.wait_ge(p2.z_in[q], n * 32 + 32)
                dve.wait_ge(p2.merged, g + 1)
                v.tensor_tensor(same[:, q, :].rearrange("p (a b) -> p a b", b=P),
                                s16b[:, q, :].rearrange("p (a b) -> p a b", b=P),
                                bc(src_f[:, ds(g * GT, GT)], P), ALU.is_equal).then_inc(p2.same_ready, 1)
                dve.wait_ge(p2.funcs_done, g + 3)
                st = stepper(dve, p2.dve_step, g * 3)
                st(v.tensor_scalar(U[:, q, :], U[:, q, :], 3.0e38, 1.0, ALU.min, ALU.add))
                st(v.reciprocal(U[:, q, :], U[:, q, :]))
                st(v.tensor_tensor(R[:, q, :], R[:, q, :], L[:, q, :], ALU.add))
                dve.wait_ge(p2.turned, g + 1)
                v.tensor_tensor(msg_t[:, q, :], U[:, q, :], R[:, q, :], ALU.mult).then_inc(p2.msg_t_ready, 1)

            def take_msg(g, q):
                dve.wait_ge(p2.turned, g + 3)
                dve.wait_ge(p2.merged, g + 1)
                v.tensor_copy(msg[:, q, :], PS[:, 2 + q, :]).then_inc(p2.msg_ready, 1)

            dve.wait_ge(norm.ready, 1)
            dve.sem_inc(p2.same_ready, 2)
            dve.sem_inc(p2.msg_t_ready, 2)
            dve.sem_inc(p2.msg_ready, 2)
            messages(0, 0, 0)
            with dve.Fori(0, NG // 2 - 1) as i:
                messages(i * 2 + 1, 1, i)
                take_msg(i * 2, 0)
                messages(i * 2 + 2, 0, i + 1)
                take_msg(i * 2 + 1, 1)
            messages(NG - 1, 1, NG // 2 - 1)
            take_msg(NG - 2, 0)
            take_msg(NG - 1, 1)

            for i in range(NI):
                q = i % 2
                st = stepper(dve, fin_step, 3 * i)
                dve.wait_ge(fin_in[q], 16 * GT * (i // 2 + 1))
                st(v.tensor_tensor(fin[:, q, 0, :], fin[:, q, 0, :], fin[:, q, 1, :], ALU.add))
                st(v.tensor_tensor(fin[:, q, 2, :], fin[:, q, 2, :], fin[:, q, 3, :], ALU.add))
                st(v.tensor_tensor(fin[:, q, 0, :], fin[:, q, 0, :], fin[:, q, 2, :], ALU.add))

        @block.tensor
        def _(pe):
            mm, turn = nc.tensor.matmul, nc.tensor.transpose
            pe.wait_ge(consts, 1)
            pe.wait_ge(in_w, 160)
            pe.wait_ge(words_in, 16)

            def place(b, j):
                return PS[:, b + j // 4, (j % 4) * F:(j % 4 + 1) * F]

            for c in range(2):
                k, n = conv[c], node[c]
                pair = pe.alloc_register(f"pe_pair{c}")
                pe.reg_mov(pair, 0)
                with pe.Fori(0, ITER) as i:
                    for s in range(SL):
                        lo, hi = windows(pe, i * SL + s)
                        pe.wait_ge(k.rows_landed[s], i * (16 * GT) + 16 * GT)
                        with pe.Fori(lo, hi):
                            m = tick(pe, pair)
                            pe.wait_ge(k.onehot_ready, m)
                            pe.wait_ge(k.sum_added, m)
                            for t in range(GT):
                                ins = mm(ps_agg, onehot[:, t, :], rows[:, s * GT + t, :],
                                         start=t == 0, stop=t == GT - 1)
                            ins.then_inc(k.sum_ready, 1)
                        pe.drain().then_inc(k.group_done, 1)
                wn, wr = (W1N, W1R) if c == 0 else (W2N, W2R)
                with pe.Fori(0, NI) as i:
                    pe.wait_ge(n.mean_ready, i + 1)
                    for j in range(NB):
                        turn(place(0, j), mean_s[:, j, :], ident[:])
                    pe.wait_ge(n.h_staged, i + 1)
                    for j in range(NB):
                        ins = turn(place(2, j), h_s[:, j, :], ident[:])
                    ins.then_inc(n.turned, 1)
                    pe.wait_ge(n.mean_t_ready, i + 1)
                    pe.wait_ge(n.h_t_ready, i + 1)
                    for j in range(NB):
                        mm(place(4, j), mean_t[:, j, :], wn[:], start=True, stop=False)
                        ins = mm(place(4, j), h_t[:, j, :], wr[:], start=False, stop=True)
                    ins.then_inc(n.product, 1)

            def pq_group(i, first=False):
                pe.wait_ge(pq.staged, i + 1)
                if not first:
                    pe.wait_ge(pq.p_ready, i)
                    pe.wait_ge(pq.rest, i * 3)
                for j in range(NB):
                    ins = turn(place(0, j), hq_s[:, j, :], ident[:])
                ins.then_inc(pq.turned, 1)
                pe.wait_ge(pq.evicted, i + 1)
                for b in (0, 4):
                    for j in range(NB):
                        ins = mm(PS[:, b + j // 2, (j % 2) * H2:(j % 2 + 1) * H2], hq_t[:, j, :],
                                 WAB[:, b // 4 * H2:(b // 4 + 1) * H2], start=True, stop=True)
                ins.then_inc(pq.product, 1)
            pq_group(0, first=True)
            with pe.Fori(1, NI) as i:
                pq_group(i)

            pe.wait_ge(pq.part, 3 * NI)
            pe.wait_ge(pq.p_ready, NI)
            pe.sem_inc(p1.done, SL)
            pe.sem_inc(p1.oht_used, 1)
            pair = pe.alloc_register("pe_pair2")
            pe.reg_mov(pair, 0)
            with pe.Fori(0, ITER) as i:
                for s in range(SL):
                    g, q, n = i * SL + s, s % 2, i * 2 + s // 2
                    lo, hi = windows(pe, g)
                    pe.wait_ge(p1.edges_landed[q], n * 32 + 32)
                    pe.wait_ge(p1.evicted, g + 1)
                    for h in range(2):
                        mm(PS[:, 2 * q + h, :], WC[:, h * F:(h + 1) * F], ebuf[:, q, :], start=True, stop=False,
                           skip_group_check=True)
                    with pe.Fori(lo, hi) as w:
                        m, w = tick(pe, pair), window(w)
                        pe.wait_ge(p1.oht_ready, m)
                        for h in range(2):
                            for j in range(3):
                                part = Q[:, j, ds(w, 1), h * F:(h + 1) * F].rearrange("p a b -> p (a b)")
                                ins = mm(PS[:, 2 * q + h, :], part, oht, start=False, stop=True,
                                         skip_group_check=True)
                        ins.then_inc(p1.oht_used, 1)
                    pe.wait_ge(p1.rows_landed[s], i * (16 * GT) + 16 * GT)
                    pe.wait_ge(p1.z_ready, g + 1)
                    for t in range(GT):
                        for h in range(2):
                            ins = turn(PS[:, 4 + 2 * q + h, t * P:(t + 1) * P],
                                       prow[:, s * GT + t, h * F:(h + 1) * F], ident[:])
                    ins.then_inc(p1.done, 1)

            def turn_msg(g, q):
                pe.wait_ge(p2.msg_t_ready, g + 3)
                pe.wait_ge(p2.msg_ready, g + 1)
                for t in range(GT):
                    ins = turn(PS[:, 2 + q, t * P:(t + 1) * P], msg_t[:, q, t * P:(t + 1) * P], ident[:])
                ins.then_inc(p2.turned, 1)

            def merge(g, q):
                pe.wait_ge(p2.msg_ready, g + 3)
                pe.wait_ge(p2.same_ready, g + 3)
                pe.wait_ge(p2.drow_ready, g + 1)
                for t in range(GT):
                    c = slice(t * P, (t + 1) * P)
                    ins = mm(PS[:, 4 + q, c], same[:, q, c], msg[:, q, c], start=True, stop=True)
                ins.then_inc(p2.merged, 1)

            pe.wait_ge(norm.ready, 1)
            pe.sem_inc(p2.turned, 2)
            pe.sem_inc(p2.merged, 2)
            turn_msg(0, 0)
            with pe.Fori(0, NG // 2 - 1) as i:
                turn_msg(i * 2 + 1, 1)
                merge(i * 2, 0)
                turn_msg(i * 2 + 2, 0)
                merge(i * 2 + 1, 1)
            turn_msg(NG - 1, 1)
            merge(NG - 2, 0)
            merge(NG - 1, 1)


def kernel(x, src, dst, edge_attr_128, L0_gnn_W1_nbr, L0_gnn_W1_root, L0_gnn_b1, L0_gnn_W2_nbr,
           L0_gnn_W2_root, L0_gnn_b2, L1_gnn_W, L1_gnn_b, L1_gnn_gamma, L1_gnn_beta):
    import numpy as np
    import concourse.bacc as bacc
    from concourse import mybir
    from concourse.bass_utils import run_bass_kernel_spmd

    P, GE = 128, 512
    N, F = x.shape
    E = src.shape[0]
    NP = -(-N // P) * P
    NG = -(-E // GE)
    EP = NG * GE

    def c(a):
        return np.ascontiguousarray(np.asarray(a))

    def padded(a, n, fill):
        a = np.asarray(a)
        return np.concatenate([a, np.full((n - a.shape[0],) + a.shape[1:], fill, a.dtype)])

    sp, dp = padded(src, EP, N), padded(dst, EP, N)
    wt = np.asarray(L1_gnn_W).T
    arrays = {
        "x": padded(x, NP, 0),
        "src_cols": c(sp.reshape(EP // P, P).T), "dst_cols": c(dp.reshape(EP // P, P).T),
        "src_rows": sp.reshape(NG, GE), "dst_rows": dp.reshape(NG, GE),
        "edge_t": c(padded(edge_attr_128, EP, 0).reshape(NG, GE, F).transpose(0, 2, 1)),
        "w1n": c(L0_gnn_W1_nbr), "w1r": c(L0_gnn_W1_root), "w2n": c(L0_gnn_W2_nbr), "w2r": c(L0_gnn_W2_root),
        "b1": c(L0_gnn_b1).reshape(1, F), "b2": c(L0_gnn_b2).reshape(1, F),
        "wab": c(np.concatenate([wt[0:F], wt[F:2 * F]], axis=1)), "wc": c(wt[2 * F:3 * F]),
        "lb": c(L1_gnn_b).reshape(1, 2 * F),
        "gamma_beta": c(np.concatenate([np.asarray(L1_gnn_gamma).reshape(2, F).T,
                                        np.asarray(L1_gnn_beta).reshape(2, F).T], axis=1)),
    }
    nc = bacc.Bacc("TRN2", target_bir_lowering=False, num_devices=1)
    args = {n: nc.dram_tensor(f"in_{n}", a.shape, mybir.dt.from_np(a.dtype), kind="ExternalInput").ap()
            for n, a in arrays.items()}
    out = nc.dram_tensor("out", (NP, F), mybir.dt.float32, kind="ExternalOutput").ap()
    build_gnn(nc, edges=E, out=out, **args)
    r = run_bass_kernel_spmd(nc, [{f"in_{n}": a for n, a in arrays.items()}], core_ids=[0])
    return r.results[0]["out"][0:N]
```

```python
import concourse.bass as bass
from concourse import mybir
from contextlib import ExitStack


def build_gnn(nc, x, src_cols, dst_cols, src_rows, dst_rows, edge_t, w1n, w1r, w2n, w2r, b1, b2,
              wab, wc, lb, gamma_beta, out, edges):
    F32, BF16, I32, I16 = mybir.dt.float32, mybir.dt.bfloat16, mybir.dt.int32, mybir.dt.int16
    ALU = mybir.AluOpType
    ACT = mybir.ActivationFunctionType
    AX = mybir.AxisListType
    ds = bass.ds

    P = 128
    NP, F = x.shape
    NT = NP // P
    NB = 7
    NI = NT // NB
    GT = 4
    GE = GT * P
    NG = edge_t.shape[0]
    TILES = NG * GT
    E = edges
    SL = 4
    ITER = NG // SL
    H2 = 2 * F
    F3 = 3 * F
    EPS = 1e-5
    assert NI * NB == NT and ITER * SL == NG and NG % 4 == 0
    HALF = NG // 2

    ctx = ExitStack()
    with ctx:
        def sb(name, shape, dt=F32):
            return ctx.enter_context(nc.sbuf_tensor(name, shape, dt))

        def dram(name, shape, dt=F32):
            return nc.dram_tensor(name, shape, dt).ap()

        def sem(name):
            return ctx.enter_context(nc.semaphore(name))

        h_tab = [dram("h0_tab", (NP, F3), BF16), dram("h1_tab", (NP, F3), BF16)]
        p_tab = dram("p_tab", (NP, H2))
        z_tab = dram("z_tab", (NG, P, 2 * GE))
        acc_tab = [dram(f"acc{k}_tab", (NP + P, F)) for k in range(GT)]
        win_tab = dram("win_tab", (NG,), I32)
        src16_tab = dram("src16_tab", (NG, GE), I16)
        dst16_tab = dram("dst16_tab", (NG, GE), I16)

        X = sb("X", [P, NT, F])
        H = sb("H", [P, NT, F])
        Q = sb("Q", [P, 3, NT, H2], BF16)
        stats = sb("stats", [P, 2, NG, 6])
        src_i = sb("src_i", [P, TILES], I32)
        src_f = sb("src_f", [P, TILES])
        dst_f = sb("dst_f", [P, TILES])
        scat_i = sb("scat_i", [P, TILES], I32)
        W1N, W1R, W2N, W2R = (sb(n, [P, F]) for n in ("W1N", "W1R", "W2N", "W2R"))
        WAB = sb("WAB", [P, 2 * H2])
        WC = sb("WC", [P, H2])
        B1, B2 = sb("B1", [P, F]), sb("B2", [P, F])
        LB = sb("LB", [P, H2])
        GB = sb("GB", [P, 4])
        iota_i = sb("iota_i", [P, F], I32)
        iota = sb("iota", [P, F])
        lower = sb("lower", [P, F])
        ident = sb("ident", [P, F])
        win_i = sb("win_i", [P, 2, NT], I32)
        wneg = sb("wneg", [P, NT])
        wpos = sb("wpos", [P, NT])
        words = sb("words", [1, NG], I32)
        cnt = sb("cnt", [P, TILES])
        idx_slot = sb("idx_slot", [P, SL * GT], I32)
        small = sb("small", [P, 8, NB])
        bn = sb("bn", [P, 24])
        ARENA = 11776
        arena = sb("arena", [P, ARENA])

        q_space = Q[:].rearrange("p a b c -> p (a b c)").bitcast(F32)

        def carve(space, at, *shape, dt=F32):
            n = 1
            for d in shape:
                n *= d
            w = n if dt in (F32, I32) else n // 2
            assert at + w <= space.shape[1], (at, w)
            v = space[:, at:at + w]
            if dt != F32:
                v = v.bitcast(dt)
            if len(shape) == 2:
                v = v.rearrange("p (a b) -> p a b", a=shape[0])
            elif len(shape) == 3:
                v = v.rearrange("p (a b c) -> p a b c", a=shape[0], b=shape[1])
            return v, at + w

        AGG, _ = carve(arena, 0, NT, F + 1)
        hq_s, a = carve(arena, 0, NB, F)
        hq_t, a = carve(arena, a, NB, F)
        p_s, a = carve(arena, a, NB, H2)
        q_s, a = carve(arena, a, NB, H2)
        prow, a = carve(arena, 0, SL * GT, H2)
        ebuf, a = carve(arena, a, SL, GE)
        d16, a = carve(arena, a, SL, GE, dt=I16)
        oht, a = carve(arena, a, GE, dt=BF16)
        zt, a = carve(arena, a, 2, 2 * GE)
        zb, a = carve(arena, a, 2, 2 * GE)
        fin, a = carve(arena, 0, 2, GT, NB * F)

        dr_i, a = carve(q_space, 0, 2, GE, dt=I32)
        sr_i, a = carve(q_space, a, 2, GE, dt=I32)
        dr16, a = carve(q_space, a, 2, GE, dt=I16)
        sr16, a = carve(q_space, a, 2, GE, dt=I16)
        dst_i, a = carve(q_space, a, TILES, dt=I32)
        gmn_i, a = carve(q_space, a, 2, dt=I32)
        gmx_i, a = carve(q_space, a, 2, dt=I32)
        gw_i, a = carve(q_space, a, 2, dt=I32)
        zero, a = carve(q_space, a, 10 * F)
        xc, a = carve(q_space, a, NB, F)
        o_s, a = carve(q_space, a, NB, F)
        rest, a = carve(q_space, a, NB, F)
        parts, a_parts = carve(q_space, a, NB, F3, dt=BF16)
        mean_s, a = carve(q_space, 0, NB, F)
        h_s, a = carve(q_space, a, NB, F)
        mean_t, a = carve(q_space, a, NB, F)
        h_t, a = carve(q_space, a, NB, F)
        RW = F3 + 2
        rows, a = carve(q_space, a_parts, SL * GT, RW, dt=BF16)
        onehot, a = carve(q_space, a, GT, P, dt=BF16)
        s16, a = carve(q_space, a, 2, GE, dt=I16)
        junk, a = carve(q_space, a, GT, P)
        zin, a = carve(q_space, 0, SL, 2 * GE)
        soft, a = carve(q_space, a, SL, 2 * GE)
        s16b, a = carve(q_space, a, SL, GE, dt=I16)
        msg_t, a = carve(q_space, a, 2, GE)
        msg, a = carve(q_space, a, 2, GE)
        same, a = carve(q_space, a, 2, GE)
        drow, a = carve(q_space, a, SL, GE)

        PS = ctx.enter_context(nc.psum_tensor("PS", [P, 8, 512], F32))
        ps_agg = PS[:, 0, 0:F + 1]

        def banks(n):
            return PS[:, n:n + 2, :].rearrange("p a b -> p (a b)")[:, 0:NB * F]

        def wide(n):
            return PS[:, n:n + 4, :].rearrange("p a b -> p (a b)")[:, 0:NB * H2]

        def bc(ap, n):
            return ap.unsqueeze(2).to_broadcast([ap.shape[0], ap.shape[1], n])

        def rep(ap, n):
            return ap.unsqueeze(1).to_broadcast([ap.shape[0], n, ap.shape[1]])

        class Sems:
            pass

        def ring(name, n):
            return [sem(f"{name}{k}") for k in range(n)]

        in_idx, in_x, in_w = sem("in_idx"), sem("in_x"), sem("in_w")
        iota_done, consts = sem("iota_done"), sem("consts")
        natural_ready = sem("natural_ready")
        natural_stored, words_in = sem("natural_stored"), sem("words_in")
        zero_ready, acc_zeroed = sem("zero_ready"), sem("acc_zeroed")
        wait_done = sem("wait_done")
        chain = sem("dve_chain")
        ln = Sems()
        ln.step, ln.var, ln.root = sem("ln_step"), sem("ln_var"), sem("ln_root")
        ln.rest, ln.part, ln.stored = sem("ln_rest"), sem("ln_part"), sem("ln_stored")
        conv, node = [], []
        for c in range(2):
            k = Sems()
            k.onehot_ready, k.sum_ready = sem(f"conv{c}_onehot_ready"), sem(f"conv{c}_sum_ready")
            k.sum_added, k.counted = sem(f"conv{c}_sum_added"), sem(f"conv{c}_counted")
            k.s16_landed = ring(f"conv{c}_s16_landed", 2)
            k.group_done, k.finished = sem(f"conv{c}_group_done"), sem(f"conv{c}_finished")
            k.idx_ready, k.rows_landed = ring(f"conv{c}_idx_ready", SL), ring(f"conv{c}_rows_landed", SL)
            conv.append(k)
            n = Sems()
            n.step, n.mean_ready, n.h_staged = sem(f"node{c}_step"), sem(f"node{c}_mean_ready"), sem(f"node{c}_h_staged")
            n.turned, n.mean_t_ready, n.h_t_ready = sem(f"node{c}_turned"), sem(f"node{c}_mean_t_ready"), sem(f"node{c}_h_t_ready")
            n.product, n.var, n.root = sem(f"node{c}_product"), sem(f"node{c}_var"), sem(f"node{c}_root")
            n.ready, n.stored = sem(f"node{c}_ready"), sem(f"node{c}_stored")
            n.rest, n.part = sem(f"node{c}_rest"), sem(f"node{c}_part")
            node.append(n)
        pq = Sems()
        pq.staged, pq.turned, pq.evicted = sem("pq_staged"), sem("pq_turned"), sem("pq_evicted")
        pq.product, pq.rest, pq.part = sem("pq_product"), sem("pq_rest"), sem("pq_part")
        pq.p_ready, pq.p_stored = sem("pq_p_ready"), sem("pq_p_stored")
        p1 = Sems()
        p1.oht_ready, p1.oht_used, p1.evicted = sem("pass1_oht_ready"), sem("pass1_oht_used"), sem("pass1_evicted")
        p1.done, p1.z_ready, p1.z_free = sem("pass1_done"), sem("pass1_z_ready"), sem("pass1_z_free")
        p1.stats_done = sem("pass1_stats_done")
        p1.idx_ready, p1.rows_landed = ring("pass1_idx_ready", SL), ring("pass1_rows_landed", SL)
        p1.edges_landed, p1.z_stored = ring("pass1_edges_landed", SL), ring("pass1_z_stored", 2)
        norm = Sems()
        norm.step, norm.var, norm.root = sem("norm_step"), sem("norm_var"), sem("norm_root")
        norm.ready = sem("norm_ready")
        p2 = Sems()
        p2.act_step, p2.dve_step = sem("pass2_act_step"), sem("pass2_dve_step")
        p2.abs_ready, p2.ln_ready, p2.soft_ready = (
            sem("pass2_abs_ready"), sem("pass2_ln_ready"), sem("pass2_soft_ready"))
        p2.gate_ready, p2.same_ready, p2.msg_t_ready = (
            sem("pass2_gate_ready"), sem("pass2_same_ready"), sem("pass2_msg_t_ready"))
        p2.turned, p2.msg_ready = sem("pass2_turned"), sem("pass2_msg_ready")
        p2.merged, p2.drow_ready = sem("pass2_merged"), sem("pass2_drow_ready")
        p2.drow_free = sem("pass2_drow_free")
        p2.z_in, p2.scattered = ring("pass2_z_in", SL), ring("pass2_scattered", GT)
        fin_in, fin_out, fin_step = ring("fin_in", 2), ring("fin_out", 2), sem("fin_step")

        def stepper(eng, s, base=0):
            n = [0]

            def step(ins):
                n[0] += 1
                ins.then_inc(s, 1)
                eng.wait_ge(s, base + n[0])
            step.n = n
            return step

        def windows(eng, g):
            word = nc.values_load(words[0:1, ds(g, 1)], engines=(eng.engine,), min_val=0,
                                  max_val=64 * (NT - 1) + NT - 1,
                                  skip_runtime_bounds_check_because="dst lies in the padded nodes")
            return eng.snap(word // 64), eng.snap(word % 64 + 1)

        def window(w):
            return nc.s_assert_within(w, 0, NT - 1,
                                      skip_runtime_bounds_check_because="dst lies in the padded nodes")

        def tick(eng, reg):
            eng.reg_add(reg, reg, 1)
            return eng.snap(reg, min_val=1, max_val=NG * NT)

        def in_turn(eng, lag, body):
            for s in range(SL):
                body(0, s)
            with eng.Fori(1, ITER) as i:
                for s in range(SL):
                    body(i, s)
            for s in range(lag):
                body(ITER, s)

        def back(i, s, n):
            i, s = (i, s - n) if s >= n else (i - 1, s - n + SL)
            if isinstance(i, int) and not 0 <= i < ITER:
                return None
            return i, s

        def rows_of(tab, i):
            return tab[ds(i * (NB * P), NB * P), :].rearrange("(j p) f -> p j f", p=P)

        def row16(tab, g):
            return tab[ds(g, 1), :].to_broadcast([P, GE])

        def square(tab, g):
            return tab[ds(g, 1)].rearrange("a p e -> (a p) e")

        block = ctx.enter_context(nc.Block())

        @block.sync
        def _(sp):
            sp.dma_start(dr_i[0:HALF], dst_rows.rearrange("(p c) e -> p c e", c=2)).then_inc(in_idx, 16)
            sp.dma_start(sr_i[0:HALF], src_rows.rearrange("(p c) e -> p c e", c=2)).then_inc(in_idx, 16)
            sp.dma_start(dst_i, dst_cols).then_inc(in_idx, 16)
            sp.dma_start(src_i[:], src_cols).then_inc(in_idx, 16)
            sp.dma_start(X[:], x.rearrange("(j p) f -> p j f", p=P)).then_inc(in_x, 16)
            for t, d in ((W1N, w1n), (W1R, w1r), (W2N, w2n), (W2R, w2r), (WC, wc), (WAB, wab),
                         (B1, b1.to_broadcast([P, F])), (B2, b2.to_broadcast([P, F])),
                         (LB, lb.to_broadcast([P, H2])), (GB, gamma_beta)):
                sp.dma_start(t[:], d).then_inc(in_w, 16)
            sp.wait_ge(natural_ready, 3)
            sp.dma_start(dst16_tab.rearrange("(p c) e -> p c e", c=2), dr16[0:HALF]).then_inc(natural_stored, 16)
            sp.dma_start(src16_tab.rearrange("(p c) e -> p c e", c=2), sr16[0:HALF]).then_inc(natural_stored, 16)
            sp.dma_start(win_tab.rearrange("(p c) -> p c", c=2), gw_i[0:HALF]).then_inc(natural_stored, 16)
            sp.wait_ge(natural_stored, 48)
            sp.dma_start(words[:], win_tab.rearrange("(a g) -> a g", a=1)).then_inc(words_in, 16)
            sp.wait_ge(zero_ready, 1)
            for k in range(1, GT):
                sp.dma_start(acc_tab[k].rearrange("(p r c) f -> p r (c f)", p=P, c=10),
                             rep(zero, 5)).then_inc(acc_zeroed, 16)
            sp.dma_start(acc_tab[0][NP:NP + P, :], zero[:, 0:F]).then_inc(acc_zeroed, 16)
            def store_parts(k, tab):
                with sp.Fori(0, NI) as i:
                    sp.wait_ge(k.part, i * 3 + 3)
                    sp.dma_start(rows_of(tab, i), parts).then_inc(k.stored, 16)

            def load_src(c):
                with sp.Fori(0, ITER) as i:
                    for j in range(2):
                        sp.wait_ge(conv[c].counted, i * (2 * GT) + (j + 1) * GT)
                        sp.dma_start(s16[:, j, :], row16(src16_tab, i * SL + 2 * j + c)
                                     ).then_inc(conv[c].s16_landed[j], 16)

            store_parts(ln, h_tab[0])
            load_src(0)
            store_parts(node[0], h_tab[1])
            load_src(1)
            with sp.Fori(0, NI) as i:
                sp.wait_ge(node[1].ready, i + 1)
                sp.dma_start(rows_of(acc_tab[0], i), X[:, ds(i * NB, NB), :]).then_inc(node[1].stored, 16)
            with sp.Fori(0, NI) as i:
                sp.wait_ge(pq.p_ready, i + 1)
                sp.dma_start(rows_of(p_tab, i), p_s).then_inc(pq.p_stored, 16)

            def load_edges(g, s):
                sp.dma_start(ebuf[:, s, :], square(edge_t, g)).then_inc(p1.edges_landed[s], 16)
                sp.dma_start(d16[:, s, :], row16(dst16_tab, g)).then_inc(p1.edges_landed[s], 16)

            sp.wait_ge(pq.p_stored, 16 * NI)
            sp.wait_ge(pq.part, 3 * NI)
            sp.sem_inc(p1.z_free, 2)
            for s in range(SL):
                load_edges(s, s)

            def edges_in_z_out(i, s):
                g, q, n = i * SL + s, s % 2, i * 2 + s // 2
                if not (isinstance(i, int) and i == ITER - 1):
                    sp.wait_ge(p1.done, g + SL + 1)
                    load_edges(g + SL, s)
                if back(i, s, 2):
                    sp.wait_ge(p1.z_stored[q], n * 16)
                    sp.sem_inc(p1.z_free, 1)
                sp.wait_ge(p1.z_ready, g + 3)
                sp.dma_start(square(z_tab, g), zb[:, q, :]).then_inc(p1.z_stored[q], 16)
            for s in range(SL):
                edges_in_z_out(0, s)
            with sp.Fori(1, ITER - 1) as i:
                for s in range(SL):
                    edges_in_z_out(i, s)
            for s in range(SL):
                edges_in_z_out(ITER - 1, s)
            for q in range(2):
                sp.wait_ge(p1.z_stored[q], 16 * (NG // 2))

            sp.wait_ge(norm.ready, 1)
            with sp.Fori(0, ITER) as i:
                for s in range(SL):
                    g = i * SL + s
                    sp.wait_ge(p2.soft_ready, g + 1)
                    sp.wait_ge(p2.same_ready, g + 1)
                    sp.dma_start(zin[:, s, :], square(z_tab, g)).then_inc(p2.z_in[s], 16)
                    sp.dma_start(s16b[:, s, :], row16(src16_tab, g)).then_inc(p2.z_in[s], 16)

            def store_out(i):
                q = i % 2
                sp.wait_ge(fin_step, 3 * (i + 1))
                sp.dma_start(rows_of(out, i), fin[:, q, 0, :].rearrange("p (j f) -> p j f", f=F)
                             ).then_inc(fin_out[q], 16)
            for k in range(GT):
                sp.wait_ge(p2.scattered[k], 16 * NG)
            for i in range(NI):
                q = i % 2
                if i >= 2:
                    sp.wait_ge(fin_out[q], 16 * (i // 2))
                for k in range(GT):
                    sp.dma_start(fin[:, q, k, :].rearrange("p (j f) -> p j f", f=F),
                                 rows_of(acc_tab[k], i)).then_inc(fin_in[q], 16)
                if i >= 1:
                    store_out(i - 1)
            store_out(NI - 1)
            sp.wait_ge(fin_out[0], 16 * ((NI + 1) // 2))
            sp.wait_ge(fin_out[1], 16 * (NI // 2))

        @block.gpsimd
        def _(pool):
            nc.gpsimd.iota(iota_i[:], pattern=[[1, F]], base=0, channel_multiplier=0).then_inc(iota_done, 1)
            nc.gpsimd.iota(win_i[:, 0, :], pattern=[[-P, NT]], base=0, channel_multiplier=0).then_inc(iota_done, 1)
            nc.gpsimd.iota(win_i[:, 1, :], pattern=[[P, NT]], base=0, channel_multiplier=1).then_inc(iota_done, 1)

            def gather_all(k, table, buf, width):
                with pool.Fori(0, ITER) as i:
                    for s in range(SL):
                        pool.wait_ge(k.idx_ready[s], i + 1)
                        pool.sem_inc(wait_done, 1)
                        for t in range(s * GT, s * GT + GT):
                            nc.gpsimd.indirect_dma_start(buf[:, t, 0:width], None, table,
                                                         bass.IndirectOffsetOnAxis(idx_slot[:, t:t + 1], 0)
                                                         ).then_inc(k.rows_landed[s], 16)

            pool.wait_ge(ln.stored, 16 * NI)
            gather_all(conv[0], h_tab[0], rows, F3)
            pool.wait_ge(node[0].stored, 16 * NI)
            gather_all(conv[1], h_tab[1], rows, F3)
            pool.wait_ge(pq.p_stored, 16 * NI)
            gather_all(p1, p_tab, prow, H2)

            def scatter(g, s, first=False):
                pool.wait_ge(p2.drow_ready, g + 3)
                for k in range(GT):
                    if not first:
                        pool.wait_ge(p2.scattered[k], g * 16)
                    pool.sem_inc(p2.drow_free if k == GT - 1 else wait_done, 1)
                    t = s * GT + k
                    nc.gpsimd.indirect_dma_start(acc_tab[k], bass.IndirectOffsetOnAxis(idx_slot[:, t:t + 1], 0),
                                                 drow[:, s, k * F:(k + 1) * F], None,
                                                 compute_op=ALU.add).then_inc(p2.scattered[k], 16)
            pool.wait_ge(acc_zeroed, 16 * GT)
            pool.wait_ge(node[1].stored, 16 * NI)
            pool.sem_inc(p2.drow_free, SL - 1)
            for s in range(SL):
                scatter(s, s, first=s == 0)
            with pool.Fori(1, ITER) as i:
                for s in range(SL):
                    scatter(i * SL + s, s)

        @block.scalar
        def _(act):
            act.wait_ge(in_idx, 64)

            def put_idx(table, g, s, signal):
                return nc.scalar.copy(idx_slot[:, s * GT:(s + 1) * GT], table[:, ds(g * GT, GT)]).then_inc(signal, 1)

            def root(k, i):
                act.wait_ge(k.var, i + 1)
                nc.scalar.activation(small[:, 3, :], small[:, 2, :], ACT.Sqrt).then_inc(k.root, 1)

            def split(k, i, first=False):
                act.wait_ge(k.rest, i * 3 + 1)
                if not first:
                    act.wait_ge(k.stored, i * 16)
                act.sem_inc(wait_done, 1)
                nc.scalar.copy(parts[:, :, 0:F], H[:, ds(i * NB, NB), :]).then_inc(k.part, 1)
                for j in (1, 2):
                    act.wait_ge(k.rest, i * 3 + j + 1)
                    nc.scalar.copy(parts[:, :, j * F:(j + 1) * F], rest).then_inc(k.part, 1)

            root(ln, 0)
            split(ln, 0, first=True)
            with act.Fori(1, NI) as i:
                root(ln, i)
                split(ln, i)

            for c in range(2):
                k, n = conv[c], node[c]
                for s in range(SL):
                    put_idx(src_i, s, s, k.idx_ready[s])
                with act.Fori(0, ITER - 1) as i:
                    for s in range(SL):
                        g = i * SL + s
                        act.wait_ge(k.group_done, g + 1)
                        put_idx(src_i, g + SL, s, k.idx_ready[s])
                act.wait_ge(k.group_done, NG)
                act.wait_ge(k.finished, 1)

                def node_group(i, first=False):
                    nc.scalar.copy(h_s, H[:, ds(i * NB, NB), :]).then_inc(n.h_staged, 1)
                    act.wait_ge(n.turned, i + 1)
                    nc.scalar.copy(h_t.rearrange("p a b -> p (a b)"), banks(2)).then_inc(n.h_t_ready, 1)
                    if c == 0:
                        split(n, i, first)
                    else:
                        root(n, i)
                node_group(0, first=True)
                with act.Fori(1, NI) as i:
                    node_group(i)

            act.wait_ge(node[1].ready, NI)
            def pq_group(i, first=False):
                nc.scalar.copy(hq_s, H[:, ds(i * NB, NB), :]).then_inc(pq.staged, 1)
                act.wait_ge(pq.product, i + 1)
                if not first:
                    act.wait_ge(pq.p_stored, i * 16)
                nc.scalar.copy(p_s.rearrange("p a b -> p (a b)"), wide(0)).then_inc(pq.p_ready, 1)
                for j in range(3):
                    act.wait_ge(pq.rest, i * 3 + j + 1)
                    nc.scalar.copy(Q[:, j, ds(i * NB, NB), :], q_s).then_inc(pq.part, 1)
            pq_group(0, first=True)
            with act.Fori(1, NI) as i:
                pq_group(i)

            def evict(g, q):
                act.wait_ge(p1.done, g + SL + 1)
                act.wait_ge(p1.z_ready, g + 1)
                nc.scalar.copy(zt[:, q, :], PS[:, 2 * q:2 * q + 2, :].rearrange("p a b -> p (a b)")
                               ).then_inc(p1.evicted, 1)
            act.wait_ge(pq.p_stored, 16 * NI)
            act.sem_inc(p1.evicted, 2)
            for s in range(SL):
                put_idx(src_i, s, s, p1.idx_ready[s])
            with act.Fori(0, ITER - 1) as i:
                for s in range(SL):
                    g = i * SL + s
                    evict(g, s % 2)
                    put_idx(src_i, g + SL, s, p1.idx_ready[s])
            for s in range(SL):
                evict(NG - SL + s, s % 2)

            act.wait_ge(norm.var, 1)
            nc.scalar.activation(bn[:, 6:8], bn[:, 4:6], ACT.Sqrt).then_inc(norm.root, 1)

            def softened(i, s):
                g = i * SL + s
                act.wait_ge(p2.abs_ready, g + 1)
                nc.scalar.activation(soft[:, s, :], soft[:, s, :], ACT.Exp, scale=-1.0).then_inc(p2.act_step, 1)
                act.wait_ge(p2.act_step, g + 1)
                nc.scalar.activation(soft[:, s, :], soft[:, s, :], ACT.Ln, bias=1.0).then_inc(p2.ln_ready, 1)

            def gate(i, s):
                g = i * SL + s
                act.wait_ge(p2.soft_ready, g + SL + 1)
                nc.scalar.activation(soft[:, s, 0:GE], soft[:, s, 0:GE], ACT.Exp, scale=-1.0
                                     ).then_inc(p2.gate_ready, 1)

            def take_msg(i, s):
                g, q = i * SL + s, s % 2
                act.wait_ge(p2.turned, g + 3)
                act.wait_ge(p2.merged, g + 1)
                nc.scalar.copy(msg[:, q, :], PS[:, 2 + q, :]).then_inc(p2.msg_ready, 1)

            def take_sums(i, s):
                g = i * SL + s
                act.wait_ge(p2.merged, g + 3)
                act.wait_ge(p2.drow_free, g + 1)
                nc.scalar.copy(drow[:, s, :], PS[:, 4 + s % 2, :])
                put_idx(scat_i, g, s, p2.drow_ready)

            def pass2(i, s):
                for n, stage in ((0, softened), (1, gate), (3, take_msg), (4, take_sums)):
                    at = back(i, s, n)
                    if at:
                        stage(*at)

            nc.scalar.preload_act_table_set("natural_log_exp_and_others")
            act.wait_ge(norm.ready, 1)
            act.sem_inc(p2.msg_ready, 2)
            act.sem_inc(p2.drow_ready, 2)
            in_turn(act, 4, pass2)

        @block.vector
        def _(dve):
            v = nc.vector
            step = stepper(dve, chain)
            dve.wait_ge(iota_done, 3)
            step(v.tensor_copy(iota[:], iota_i[:]))
            step(v.tensor_copy(wneg[:], win_i[:, 0, :]))
            step(v.tensor_copy(wpos[:], win_i[:, 1, :]))
            step(v.tensor_scalar(ident[:], iota[:], wpos[:, 0:1], None, ALU.is_equal))
            v.tensor_scalar(lower[:], iota[:], wpos[:, 0:1], None, ALU.is_lt).then_inc(consts, 1)
            v.memset(zero, 0.0).then_inc(zero_ready, 1)
            dve.wait_ge(in_idx, 64)
            d, s_ = dr_i[0:HALF], sr_i[0:HALF]
            v.tensor_copy(dr16[0:HALF], d).then_inc(natural_ready, 1)
            v.tensor_copy(sr16[0:HALF], s_).then_inc(natural_ready, 1)
            step(v.tensor_reduce(gmn_i[0:HALF], d, AX.X, ALU.min))
            step(v.tensor_reduce(gmx_i[0:HALF], d, AX.X, ALU.max))
            step(v.tensor_scalar(gmn_i[0:HALF], gmn_i[0:HALF], 7, None, ALU.logical_shift_right))
            step(v.tensor_scalar(gmx_i[0:HALF], gmx_i[0:HALF], 7, None, ALU.logical_shift_right))
            v.scalar_tensor_tensor(gw_i[0:HALF], gmn_i[0:HALF], 64.0, gmx_i[0:HALF], ALU.mult, ALU.add
                                   ).then_inc(natural_ready, 1)
            step(v.tensor_copy(src_f[:], src_i[:]))
            step(v.tensor_copy(dst_f[:], dst_i))

            def split(k, i, hs):
                for j in range(2):
                    dve.wait_ge(k.part, i * 3 + j + 1)
                    v.tensor_tensor(rest, rest if j else hs, parts[:, :, j * F:(j + 1) * F], ALU.subtract
                                    ).then_inc(k.rest, 1)

            def inverse_root(step, var, root, inv, tmp):
                step(v.reciprocal(inv, root))
                step(v.tensor_tensor(tmp, inv, inv, ALU.mult))
                step(v.tensor_tensor(tmp, tmp, var, ALU.mult))
                step(v.tensor_scalar(tmp, tmp, -0.5, 1.5, ALU.mult, ALU.add))
                step(v.tensor_tensor(inv, inv, tmp, ALU.mult))

            def layer_norm(i, step, var_ready, root, out_h):
                xs = X[:, ds(i * NB, NB), :]
                dve.sem_inc(wait_done, 1)
                step(v.tensor_reduce(small[:, 0, :], xs, AX.X, ALU.add))
                step(v.tensor_scalar(small[:, 1, :], small[:, 0, :], -1.0 / F, None, ALU.mult))
                step(v.tensor_tensor(xc, xs, bc(small[:, 1, :], F), ALU.add))
                step(v.tensor_tensor(o_s, xc, xc, ALU.mult))
                step(v.tensor_reduce(small[:, 0, :], o_s, AX.X, ALU.add))
                v.tensor_scalar(small[:, 2, :], small[:, 0, :], 1.0 / F, EPS, ALU.mult, ALU.add
                                ).then_inc(var_ready, 1)
                dve.wait_ge(root, i + 1)
                inverse_root(step, small[:, 2, :], small[:, 3, :], small[:, 4, :], small[:, 5, :])
                return v.scalar_tensor_tensor(out_h, xc, 0.0, bc(small[:, 4, :], F), ALU.max, ALU.mult)

            dve.wait_ge(in_x, 16)
            LN_STEPS = 10
            with dve.Fori(0, NI) as i:
                st = stepper(dve, ln.step, i * LN_STEPS)
                hs = H[:, ds(i * NB, NB), :]
                layer_norm(i, st, ln.var, ln.root, hs).then_inc(ln.rest, 1)
                split(ln, i, hs)
                assert st.n[0] == LN_STEPS

            def sum_by_window(k, g, pair):
                lo, hi = windows(dve, g)
                with dve.Fori(lo, hi) as w:
                    n, w = tick(dve, pair), window(w)
                    v.scalar_tensor_tensor(onehot, bc(dst_f[:, ds(g * GT, GT)], P), wneg[:, ds(w, 1)],
                                           rep(iota[:], GT), ALU.add, ALU.is_equal).then_inc(k.onehot_ready, 1)
                    dve.wait_ge(k.sum_ready, n)
                    dve.wait_ge(k.sum_added, n)
                    a = AGG[:, ds(w, 1), :].rearrange("p a b -> p (a b)")
                    v.tensor_tensor(a, a, ps_agg, ALU.add).then_inc(k.sum_added, 1)

            def count_repeats(k, g, j, i):
                dve.wait_ge(k.s16_landed[j], i * 16 + 16)
                dve.wait_ge(k.counted, i * (2 * GT) + (j + 1) * GT + GT)
                for t in range(GT):
                    v.scalar_tensor_tensor(junk[:, t, :], s16[:, j, t * P:(t + 1) * P],
                                           src_f[:, ds(g * GT + t, 1)], lower[:], ALU.is_equal, ALU.mult,
                                           accum_out=cnt[:, ds(g * GT + t, 1)]).then_inc(k.counted, 1)

            dve.wait_ge(natural_stored, 48)
            dve.wait_ge(words_in, 16)
            NODE_STEPS = [3, 15]
            for c in range(2):
                k, n = conv[c], node[c]
                v.memset(AGG, 0.0).then_inc(k.sum_added, 1)
                if c == 0:
                    step(v.memset(rows[:, :, F3:F3 + 2], 1.0))
                pair = dve.alloc_register(f"dve_pair{c}")
                dve.reg_mov(pair, 0)
                dve.sem_inc(k.counted, 2 * GT)
                with dve.Fori(0, ITER) as i:
                    for s in range(SL):
                        sum_by_window(k, i * SL + s, pair)
                        if s % 2 == c:
                            count_repeats(k, i * SL + s, s // 2, i)
                dve.wait_ge(k.group_done, NG)
                dve.wait_ge(k.sum_added, tick(dve, pair))
                if c == 1:
                    dve.wait_ge(k.counted, (NG // 2 + 2) * GT)
                    big, _ = carve(q_space, 0, TILES)
                    step(v.tensor_scalar(bn[:, 0:1], wpos[:, 0:1], float(NP), None, ALU.add))
                    step(v.tensor_scalar(big, src_f[:], -1.0, bn[:, 0:1], ALU.mult, ALU.add))
                    step(v.tensor_scalar(cnt[:], cnt[:], 0.0, None, ALU.is_gt))
                    step(v.tensor_tensor(big, big, cnt[:], ALU.mult))
                    step(v.tensor_tensor(scat_i[:], big, src_f[:], ALU.add))
                dve.wait_ge(acc_zeroed, 16 * GT)
                dve.sem_inc(k.finished, 1)
                with dve.Fori(0, NI) as i:
                    st = stepper(dve, n.step, i * NODE_STEPS[c])
                    deg = AGG[:, ds(i * NB, NB), F:F + 1].rearrange("p a b -> p (a b)")
                    st(v.tensor_scalar(small[:, 6, :], deg, 1.0, None, ALU.max))
                    st(v.reciprocal(small[:, 7, :], small[:, 6, :]))
                    v.tensor_tensor(mean_s, AGG[:, ds(i * NB, NB), 0:F], bc(small[:, 7, :], F), ALU.mult
                                    ).then_inc(n.mean_ready, 1)
                    dve.wait_ge(n.turned, i + 1)
                    v.tensor_copy(mean_t.rearrange("p a b -> p (a b)"), banks(0)).then_inc(n.mean_t_ready, 1)
                    dve.wait_ge(n.product, i + 1)
                    hs, xs = H[:, ds(i * NB, NB), :], X[:, ds(i * NB, NB), :]
                    product = banks(4).rearrange("p (a b) -> p a b", b=F)
                    st(v.tensor_tensor(o_s, product, rep((B1 if c == 0 else B2)[:], NB), ALU.add))
                    if c == 0:
                        v.tensor_scalar(hs, o_s, 0.0, None, ALU.max).then_inc(n.rest, 1)
                        split(n, i, hs)
                    else:
                        st(v.tensor_tensor(xs, xs, o_s, ALU.add))
                        st(layer_norm(i, st, n.var, n.root, hs))
                        v.tensor_tensor(xs, xs, hs, ALU.add).then_inc(n.ready, 1)
                        dve.wait_ge(n.ready, i + 1)
                    assert st.n[0] == NODE_STEPS[c], st.n

            with dve.Fori(0, NI) as i:
                dve.wait_ge(pq.turned, i + 1)
                v.tensor_copy(hq_t.rearrange("p a b -> p (a b)"), banks(0)).then_inc(pq.evicted, 1)
                dve.wait_ge(pq.product, i + 1)
                v.tensor_tensor(q_s, wide(4).rearrange("p (a b) -> p a b", b=H2), rep(LB[:], NB), ALU.add
                                ).then_inc(pq.rest, 1)
                for j in range(2):
                    dve.wait_ge(pq.part, i * 3 + j + 1)
                    v.tensor_tensor(q_s, q_s, Q[:, j, ds(i * NB, NB), :], ALU.subtract).then_inc(pq.rest, 1)
                dve.wait_ge(pq.part, i * 3 + 3)

            def onehot_by_window(i, s, pair):
                lo, hi = windows(dve, i * SL + s)
                dve.wait_ge(p1.edges_landed[s], i * 32 + 32)
                with dve.Fori(lo, hi) as w:
                    m, w = tick(dve, pair), window(w)
                    dve.wait_ge(p1.oht_used, m)
                    v.tensor_scalar(oht, d16[:, s, :], wpos[:, ds(w, 1)], None, ALU.is_equal
                                    ).then_inc(p1.oht_ready, 1)

            def finish_z(g, q, valid=GE):
                dve.wait_ge(p1.evicted, g + 3)
                dve.wait_ge(p1.z_free, g + 1)
                dve.wait_ge(p1.stats_done, g + 1)
                v.tensor_tensor(zb[:, q, :], zt[:, q, :], PS[:, 4 + 2 * q:6 + 2 * q, :].rearrange("p a b -> p (a b)"),
                                ALU.add).then_inc(p1.z_ready, 1)
                dve.wait_ge(p1.z_ready, g + 3)
                for h in range(2):
                    ins = v.bn_stats(stats[:, h, ds(g, 1), :].rearrange("p a b -> p (a b)"),
                                     zb[:, q, h * GE:h * GE + valid])
                ins.then_inc(p1.stats_done, 1)

            dve.wait_ge(pq.p_stored, 16 * NI)
            dve.sem_inc(p1.z_ready, 2)
            dve.sem_inc(p1.stats_done, 2)
            pair = dve.alloc_register("dve_pair2")
            dve.reg_mov(pair, 0)

            def pass1(i, s):
                if back(i, s, 0):
                    onehot_by_window(i, s, pair)
                at = back(i, s, 1)
                if at:
                    g = at[0] * SL + at[1]
                    finish_z(g, at[1] % 2, E - g * GE if isinstance(g, int) and g == NG - 1 else GE)
            in_turn(dve, 1, pass1)
            dve.wait_ge(p1.stats_done, NG + 2)

            nst = stepper(dve, norm.step)
            for h in range(2):
                nst(v.bn_aggr(bn[:, 2 * h:2 * h + 2], stats[:, h].rearrange("p a b -> p (a b)")))
            mv = bn[:, 0:4].rearrange("p (h k) -> p k h", k=2)
            v.tensor_scalar(bn[:, 4:6], mv[:, 1, :], EPS, None, ALU.add).then_inc(norm.var, 1)
            dve.wait_ge(norm.root, 1)
            inverse_root(nst, bn[:, 4:6], bn[:, 6:8], bn[:, 14:16], bn[:, 16:18])
            nst(v.tensor_tensor(bn[:, 8:10], bn[:, 14:16], GB[:, 0:2], ALU.mult))
            nst(v.tensor_tensor(bn[:, 18:20], mv[:, 0, :], bn[:, 8:10], ALU.mult))
            nst(v.tensor_tensor(bn[:, 10:12], GB[:, 2:4], bn[:, 18:20], ALU.subtract))
            nst(v.tensor_scalar(bn[:, 12:13], bn[:, 8:9], -1.0, None, ALU.mult))
            v.tensor_scalar(bn[:, 13:14], bn[:, 10:11], -1.0, None, ALU.mult).then_inc(norm.ready, 1)

            def take_z(i, s):
                g = i * SL + s
                dve.wait_ge(p2.z_in[s], i * 32 + 32)
                v.tensor_scalar(zin[:, s, 0:GE], zin[:, s, 0:GE], bn[:, 12:13], bn[:, 13:14], ALU.mult, ALU.add
                                ).then_inc(p2.dve_step, 1)
                v.tensor_scalar(zin[:, s, GE:2 * GE], zin[:, s, GE:2 * GE], bn[:, 9:10], bn[:, 11:12],
                                ALU.mult, ALU.add).then_inc(p2.dve_step, 1)
                dve.wait_ge(p2.dve_step, g * 2 + 2)
                v.scalar_tensor_tensor(soft[:, s, :], zin[:, s, :], -1.0, zin[:, s, :], ALU.mult, ALU.max
                                       ).then_inc(p2.abs_ready, 1)

            def soften(i, s):
                g = i * SL + s
                dve.wait_ge(p2.ln_ready, g + 1)
                v.scalar_tensor_tensor(soft[:, s, :], zin[:, s, :], 0.0, soft[:, s, :], ALU.max, ALU.add
                                       ).then_inc(p2.soft_ready, 1)

            def message(i, s):
                g, q = i * SL + s, s % 2
                dve.wait_ge(p2.merged, g + 1)
                v.tensor_tensor(same[:, q, :].rearrange("p (a b) -> p a b", b=P),
                                s16b[:, s, :].rearrange("p (a b) -> p a b", b=P),
                                bc(src_f[:, ds(g * GT, GT)], P), ALU.is_equal).then_inc(p2.same_ready, 1)
                dve.wait_ge(p2.gate_ready, g + 1)
                dve.wait_ge(p2.turned, g + 1)
                v.tensor_tensor(msg_t[:, q, :], soft[:, s, 0:GE], soft[:, s, GE:2 * GE], ALU.mult
                                ).then_inc(p2.msg_t_ready, 1)

            def pass2(i, s):
                for n, stage in ((0, take_z), (1, soften), (2, message)):
                    at = back(i, s, n)
                    if at:
                        stage(*at)

            dve.wait_ge(norm.ready, 1)
            dve.sem_inc(p2.soft_ready, SL)
            dve.sem_inc(p2.same_ready, SL)
            dve.sem_inc(p2.msg_t_ready, 2)
            in_turn(dve, 2, pass2)

            for i in range(NI):
                q = i % 2
                st = stepper(dve, fin_step, 3 * i)
                dve.wait_ge(fin_in[q], 16 * GT * (i // 2 + 1))
                st(v.tensor_tensor(fin[:, q, 0, :], fin[:, q, 0, :], fin[:, q, 1, :], ALU.add))
                st(v.tensor_tensor(fin[:, q, 2, :], fin[:, q, 2, :], fin[:, q, 3, :], ALU.add))
                st(v.tensor_tensor(fin[:, q, 0, :], fin[:, q, 0, :], fin[:, q, 2, :], ALU.add))

        @block.tensor
        def _(pe):
            mm, turn = nc.tensor.matmul, nc.tensor.transpose
            pe.wait_ge(consts, 1)
            pe.wait_ge(in_w, 160)
            pe.wait_ge(words_in, 16)

            def place(b, j):
                return PS[:, b + j // 4, (j % 4) * F:(j % 4 + 1) * F]

            for c in range(2):
                k, n = conv[c], node[c]
                pair = pe.alloc_register(f"pe_pair{c}")
                pe.reg_mov(pair, 0)
                with pe.Fori(0, ITER) as i:
                    for s in range(SL):
                        lo, hi = windows(pe, i * SL + s)
                        pe.wait_ge(k.rows_landed[s], i * (16 * GT) + 16 * GT)
                        with pe.Fori(lo, hi):
                            m = tick(pe, pair)
                            pe.wait_ge(k.onehot_ready, m)
                            pe.wait_ge(k.sum_added, m)
                            for t in range(GT):
                                r = rows[:, s * GT + t, :]
                                mm(ps_agg, onehot[:, t, :], r[:, 2 * F:F3 + 1], start=t == 0, stop=False,
                                   skip_group_check=True)
                                for j in (1, 0):
                                    ins = mm(ps_agg[:, 0:F], onehot[:, t, :], r[:, j * F:(j + 1) * F],
                                             start=False, stop=t == GT - 1 and j == 0, skip_group_check=True)
                            ins.then_inc(k.sum_ready, 1)
                        pe.drain().then_inc(k.group_done, 1)
                wn, wr = (W1N, W1R) if c == 0 else (W2N, W2R)
                with pe.Fori(0, NI) as i:
                    pe.wait_ge(n.mean_ready, i + 1)
                    for j in range(NB):
                        turn(place(0, j), mean_s[:, j, :], ident[:])
                    pe.wait_ge(n.h_staged, i + 1)
                    for j in range(NB):
                        ins = turn(place(2, j), h_s[:, j, :], ident[:])
                    ins.then_inc(n.turned, 1)
                    pe.wait_ge(n.mean_t_ready, i + 1)
                    pe.wait_ge(n.h_t_ready, i + 1)
                    for j in range(NB):
                        mm(place(4, j), mean_t[:, j, :], wn[:], start=True, stop=False)
                        ins = mm(place(4, j), h_t[:, j, :], wr[:], start=False, stop=True)
                    ins.then_inc(n.product, 1)

            def pq_group(i, first=False):
                pe.wait_ge(pq.staged, i + 1)
                if not first:
                    pe.wait_ge(pq.p_ready, i)
                    pe.wait_ge(pq.rest, i * 3)
                for j in range(NB):
                    ins = turn(place(0, j), hq_s[:, j, :], ident[:])
                ins.then_inc(pq.turned, 1)
                pe.wait_ge(pq.evicted, i + 1)
                for b in (0, 4):
                    for j in range(NB):
                        ins = mm(PS[:, b + j // 2, (j % 2) * H2:(j % 2 + 1) * H2], hq_t[:, j, :],
                                 WAB[:, b // 4 * H2:(b // 4 + 1) * H2], start=True, stop=True)
                ins.then_inc(pq.product, 1)
            pq_group(0, first=True)
            with pe.Fori(1, NI) as i:
                pq_group(i)

            pe.wait_ge(pq.part, 3 * NI)
            pe.wait_ge(pq.p_ready, NI)
            pe.sem_inc(p1.done, SL)
            pe.sem_inc(p1.oht_used, 1)
            pair = pe.alloc_register("pe_pair2")
            pe.reg_mov(pair, 0)
            with pe.Fori(0, ITER) as i:
                for s in range(SL):
                    g, q = i * SL + s, s % 2
                    lo, hi = windows(pe, g)
                    pe.wait_ge(p1.edges_landed[s], i * 32 + 32)
                    pe.wait_ge(p1.evicted, g + 1)
                    for h in range(2):
                        mm(PS[:, 2 * q + h, :], WC[:, h * F:(h + 1) * F], ebuf[:, s, :], start=True, stop=False,
                           skip_group_check=True)
                    with pe.Fori(lo, hi) as w:
                        m, w = tick(pe, pair), window(w)
                        pe.wait_ge(p1.oht_ready, m)
                        for h in range(2):
                            for j in range(3):
                                part = Q[:, j, ds(w, 1), h * F:(h + 1) * F].rearrange("p a b -> p (a b)")
                                ins = mm(PS[:, 2 * q + h, :], part, oht, start=False, stop=True,
                                         skip_group_check=True)
                        ins.then_inc(p1.oht_used, 1)
                    pe.wait_ge(p1.rows_landed[s], i * (16 * GT) + 16 * GT)
                    pe.wait_ge(p1.z_ready, g + 1)
                    for t in range(GT):
                        for h in range(2):
                            ins = turn(PS[:, 4 + 2 * q + h, t * P:(t + 1) * P],
                                       prow[:, s * GT + t, h * F:(h + 1) * F], ident[:])
                    ins.then_inc(p1.done, 1)

            def turn_msg(i, s):
                g, q = i * SL + s, s % 2
                pe.wait_ge(p2.msg_t_ready, g + 3)
                pe.wait_ge(p2.msg_ready, g + 1)
                for t in range(GT):
                    ins = turn(PS[:, 2 + q, t * P:(t + 1) * P], msg_t[:, q, t * P:(t + 1) * P], ident[:])
                ins.then_inc(p2.turned, 1)

            def merge(i, s):
                g, q = i * SL + s, s % 2
                pe.wait_ge(p2.msg_ready, g + 3)
                pe.wait_ge(p2.same_ready, g + SL + 1)
                pe.wait_ge(p2.drow_ready, g + 1)
                for t in range(GT):
                    c = slice(t * P, (t + 1) * P)
                    ins = mm(PS[:, 4 + q, c], same[:, q, c], msg[:, q, c], start=True, stop=True)
                ins.then_inc(p2.merged, 1)

            def pass2(i, s):
                for n, stage in ((0, turn_msg), (1, merge)):
                    at = back(i, s, n)
                    if at:
                        stage(*at)

            pe.wait_ge(norm.ready, 1)
            pe.sem_inc(p2.turned, 2)
            pe.sem_inc(p2.merged, 2)
            in_turn(pe, 1, pass2)


def kernel(x, src, dst, edge_attr_128, L0_gnn_W1_nbr, L0_gnn_W1_root, L0_gnn_b1, L0_gnn_W2_nbr,
           L0_gnn_W2_root, L0_gnn_b2, L1_gnn_W, L1_gnn_b, L1_gnn_gamma, L1_gnn_beta):
    import numpy as np
    import concourse.bacc as bacc
    from concourse import mybir
    from concourse.bass_utils import run_bass_kernel_spmd

    P, GE = 128, 512
    N, F = x.shape
    E = src.shape[0]
    NP = -(-N // P) * P
    NG = -(-E // GE)
    EP = NG * GE

    def c(a):
        return np.ascontiguousarray(np.asarray(a))

    def padded(a, n, fill):
        a = np.asarray(a)
        return np.concatenate([a, np.full((n - a.shape[0],) + a.shape[1:], fill, a.dtype)])

    sp, dp = padded(src, EP, N), padded(dst, EP, N)
    wt = np.asarray(L1_gnn_W).T
    arrays = {
        "x": padded(x, NP, 0),
        "src_cols": c(sp.reshape(EP // P, P).T), "dst_cols": c(dp.reshape(EP // P, P).T),
        "src_rows": sp.reshape(NG, GE), "dst_rows": dp.reshape(NG, GE),
        "edge_t": c(padded(edge_attr_128, EP, 0).reshape(NG, GE, F).transpose(0, 2, 1)),
        "w1n": c(L0_gnn_W1_nbr), "w1r": c(L0_gnn_W1_root), "w2n": c(L0_gnn_W2_nbr), "w2r": c(L0_gnn_W2_root),
        "b1": c(L0_gnn_b1).reshape(1, F), "b2": c(L0_gnn_b2).reshape(1, F),
        "wab": c(np.concatenate([wt[0:F], wt[F:2 * F]], axis=1)), "wc": c(wt[2 * F:3 * F]),
        "lb": c(L1_gnn_b).reshape(1, 2 * F),
        "gamma_beta": c(np.concatenate([np.asarray(L1_gnn_gamma).reshape(2, F).T,
                                        np.asarray(L1_gnn_beta).reshape(2, F).T], axis=1)),
    }
    nc = bacc.Bacc("TRN2", target_bir_lowering=False, num_devices=1)
    args = {n: nc.dram_tensor(f"in_{n}", a.shape, mybir.dt.from_np(a.dtype), kind="ExternalInput").ap()
            for n, a in arrays.items()}
    out = nc.dram_tensor("out", (NP, F), mybir.dt.float32, kind="ExternalOutput").ap()
    build_gnn(nc, edges=E, out=out, **args)
    r = run_bass_kernel_spmd(nc, [{f"in_{n}": a for n, a in arrays.items()}], core_ids=[0])
    return r.results[0]["out"][0:N]
```

```python
import concourse.bass as bass
from concourse import mybir
from contextlib import ExitStack


def build_gnn(nc, x, src_cols, dst_cols, src_rows, dst_rows, edge_t, w1n, w1r, w2n, w2r, b1, b2,
              wab, wc, lb, gamma_beta, out, edges):
    F32, BF16, I32, I16 = mybir.dt.float32, mybir.dt.bfloat16, mybir.dt.int32, mybir.dt.int16
    ALU = mybir.AluOpType
    ACT = mybir.ActivationFunctionType
    AX = mybir.AxisListType
    ds = bass.ds

    P = 128
    NP, F = x.shape
    NT = NP // P
    NB = 7
    NI = NT // NB
    GT = 4
    GE = GT * P
    NG = edge_t.shape[0]
    TILES = NG * GT
    E = edges
    SL = 4
    ITER = NG // SL
    ACC_OF = [n % 5 for n in range(SL * GT - 1)] + [5]
    ACCS = max(ACC_OF) + 1
    H2 = 2 * F
    F3 = 3 * F
    EPS = 1e-5
    SUBS = [(0, 3), (3, 5), (5, 7)]
    CH = len(SUBS) * NI
    assert NI * NB == NT and ITER * SL == NG and NG % 4 == 0 and NT == ITER
    HALF = NG // 2

    ctx = ExitStack()
    with ctx:
        def sb(name, shape, dt=F32):
            return ctx.enter_context(nc.sbuf_tensor(name, shape, dt))

        def dram(name, shape, dt=F32):
            return nc.dram_tensor(name, shape, dt).ap()

        def sem(name):
            return ctx.enter_context(nc.semaphore(name))

        h_tab = [dram("h0_tab", (NP, F3), BF16), dram("h1_tab", (NP, F3), BF16)]
        p_tab = dram("p_tab", (NP, H2))
        z_tab = dram("z_tab", (NG, P, 2 * GE))
        acc_tab = [dram(f"acc{k}_tab", (NP + P, F)) for k in range(ACCS)]
        win_tab = dram("win_tab", (NG,), I32)
        src16_tab = dram("src16_tab", (NG, GE), I16)
        dst16_tab = dram("dst16_tab", (NG, GE), I16)

        X = sb("X", [P, NT, F])
        H = sb("H", [P, NT, F])
        Q = sb("Q", [P, 3, NT, H2], BF16)
        stats = sb("stats", [P, 2, NG, 6])
        src_i = sb("src_i", [P, TILES], I32)
        src_f = sb("src_f", [P, TILES])
        dst_f = sb("dst_f", [P, TILES])
        scat_i = sb("scat_i", [P, TILES], I32)
        W1N, W1R, W2N, W2R = (sb(n, [P, F]) for n in ("W1N", "W1R", "W2N", "W2R"))
        WAB = sb("WAB", [P, 2 * H2])
        WC = sb("WC", [P, H2])
        B1, B2 = sb("B1", [P, F]), sb("B2", [P, F])
        LB = sb("LB", [P, 2])
        GB = sb("GB", [P, 4])
        iota_i = sb("iota_i", [P, F], I32)
        iota = sb("iota", [P, F])
        lower = sb("lower", [P, F])
        ident = sb("ident", [P, F])
        win_i = sb("win_i", [P, 2, NT], I32)
        wneg = sb("wneg", [P, NT])
        wpos = sb("wpos", [P, NT])
        words = sb("words", [1, NG], I32)
        cnt = sb("cnt", [P, TILES])
        idx_slot = sb("idx_slot", [P, SL * GT], I32)
        inv_deg = sb("inv_deg", [P, NT])
        ones = sb("ones", [P, P])
        ones_bf = sb("ones_bf", [P, 2], BF16)
        bn = sb("bn", [P, 24])
        ARENA = 11776
        arena = sb("arena", [P, ARENA])

        q_space = Q[:].rearrange("p a b c -> p (a b c)").bitcast(F32)

        def carve(space, at, *shape, dt=F32):
            n = 1
            for d in shape:
                n *= d
            w = n if dt in (F32, I32) else n // 2
            assert at + w <= space.shape[1], (at, w)
            v = space[:, at:at + w]
            if dt != F32:
                v = v.bitcast(dt)
            if len(shape) == 2:
                v = v.rearrange("p (a b) -> p a b", a=shape[0])
            elif len(shape) == 3:
                v = v.rearrange("p (a b c) -> p a b c", a=shape[0], b=shape[1])
            return v, at + w

        AGG, _ = carve(arena, 0, NT, F + 1)
        qr, a = carve(arena, SL * GT * H2, 2, 3 * H2)
        p_s, a = carve(arena, NT * (F + 1), 2, NB * H2)
        ht, a = carve(arena, a, 2, NB * F)
        prow, a = carve(arena, 0, SL * GT, H2)
        ebuf, a = carve(arena, a, SL, GE)
        d16, a = carve(arena, a, SL, GE, dt=I16)
        oht, a = carve(arena, a, 2, GE, dt=BF16)
        zt, a = carve(arena, a, 2, 2 * GE)
        zb, a = carve(arena, a, 2, 2 * GE)

        dr_i, a = carve(q_space, 0, 2, GE, dt=I32)
        sr_i, a = carve(q_space, a, 2, GE, dt=I32)
        dr16, a = carve(q_space, a, 2, GE, dt=I16)
        sr16, a = carve(q_space, a, 2, GE, dt=I16)
        dst_i, a = carve(q_space, a, TILES, dt=I32)
        gmn_i, a = carve(q_space, a, 2, dt=I32)
        gmx_i, a = carve(q_space, a, 2, dt=I32)
        gw_i, a = carve(q_space, a, 2, dt=I32)
        zero, a = carve(q_space, a, F)
        stat, a = carve(q_space, a, 6, NT)
        o_s, a = carve(q_space, a, 2, NB * F)
        rest, a = carve(q_space, a, 3, NB * F)
        parts, _ = carve(q_space, a, 5, NB * F3, dt=BF16)
        a = a + 3 * NB * F3 // 2
        rows, a = carve(q_space, a, SL * GT, F3, dt=BF16)
        onehot, a = carve(q_space, a, 2, GE, dt=BF16)
        s16, a = carve(q_space, a, 2, GE, dt=I16)
        junk, a = carve(q_space, a, 2, P)
        hs, a = carve(q_space, a, F)
        hst, a = carve(q_space, a, F)
        zin, a = carve(q_space, 0, SL, 2 * GE)
        soft, a = carve(q_space, a, SL, 2 * GE)
        s16b, a = carve(q_space, a, SL, GE, dt=I16)
        msg_t, a = carve(q_space, a, 2, GE)
        msg, a = carve(q_space, a, 2, GE)
        same, a = carve(q_space, a, 2, GE)
        drow, a = carve(q_space, a, SL, GE)
        fin, a = carve(q_space, 0, 3, ACCS * NB * F)

        PS = ctx.enter_context(nc.psum_tensor("PS", [P, 8, 512], F32))
        ps_agg = PS[:, 0, 0:F + 1]

        def banks(n):
            return PS[:, n:n + 2, :].rearrange("p a b -> p (a b)")[:, 0:NB * F]

        def bc(ap, n):
            return ap.unsqueeze(2).to_broadcast([ap.shape[0], ap.shape[1], n])

        def rep(ap, n):
            return ap.unsqueeze(1).to_broadcast([ap.shape[0], n, ap.shape[1]])

        class Sems:
            pass

        def ring(name, n):
            return [sem(f"{name}{k}") for k in range(n)]

        def split_sems(k, name):
            k.source = sem(f"{name}_source")
            k.part, k.rest = ring(f"{name}_part", 3), ring(f"{name}_rest", 2)
            k.stored = ring(f"{name}_stored", 5)

        def norm_sems(k, name):
            k.centred, k.squared = sem(f"{name}_centred"), sem(f"{name}_squared")
            k.squares_used = sem(f"{name}_squares_used")
            k.var, k.root = sem(f"{name}_var"), sem(f"{name}_root")

        in_idx, in_x, in_w = sem("in_idx"), ring("in_x", NI), sem("in_w")
        iota_done, consts = sem("iota_done"), sem("consts")
        natural_ready = sem("natural_ready")
        natural_stored, words_in = sem("natural_stored"), sem("words_in")
        zero_ready, acc_zeroed = sem("zero_ready"), sem("acc_zeroed")
        wait_done = sem("wait_done")
        floats_ready = sem("floats_ready")
        chain = sem("dve_chain")
        ln = Sems()
        split_sems(ln, "ln")
        norm_sems(ln, "ln")
        agg_zeroed = sem("agg_zeroed")
        idx_ready, rows_landed = ring("idx_ready", SL), ring("rows_landed", SL)
        conv, node = [], []
        for c in range(2):
            k = Sems()
            k.onehot_ready, k.sum_ready = sem(f"conv{c}_onehot_ready"), sem(f"conv{c}_sum_ready")
            k.sum_added, k.counted = sem(f"conv{c}_sum_added"), sem(f"conv{c}_counted")
            k.s16_landed = ring(f"conv{c}_s16_landed", 2)
            k.group_done = sem(f"conv{c}_group_done")
            conv.append(k)
            n = Sems()
            n.product = sem(f"node{c}_product")
            if c == 0:
                split_sems(n, "node0")
            else:
                norm_sems(n, "node1")
                n.x_ready, n.h_ready, n.stored = sem("node1_x_ready"), sem("node1_h_ready"), sem("node1_stored")
            n.root_staged, n.root_turned = sem(f"root{c}_staged"), sem(f"root{c}_turned")
            n.root_lhs, n.root_product, n.root_done = (
                sem(f"root{c}_lhs"), sem(f"root{c}_product"), sem(f"root{c}_done"))
            node.append(n)
        pq = Sems()
        pq.turned, pq.evicted, pq.product = sem("pq_turned"), sem("pq_evicted"), sem("pq_product")
        pq.p_ready, pq.p_stored = sem("pq_p_ready"), ring("pq_p_stored", 2)
        pq.part, pq.rest = ring("pq_part", 3), ring("pq_rest", 2)
        p1 = Sems()
        p1.oht_ready, p1.oht_used, p1.evicted = sem("pass1_oht_ready"), sem("pass1_oht_used"), sem("pass1_evicted")
        p1.done, p1.z_ready, p1.z_free = sem("pass1_done"), sem("pass1_z_ready"), sem("pass1_z_free")
        p1.stats_done = sem("pass1_stats_done")
        p1.edges_landed, p1.z_stored = ring("pass1_edges_landed", SL), ring("pass1_z_stored", 2)
        norm = Sems()
        norm.step, norm.var, norm.root = sem("norm_step"), sem("norm_var"), sem("norm_root")
        norm.ready = sem("norm_ready")
        p2 = Sems()
        p2.act_step, p2.dve_step = sem("pass2_act_step"), sem("pass2_dve_step")
        p2.abs_ready, p2.ln_ready, p2.soft_ready = (
            sem("pass2_abs_ready"), sem("pass2_ln_ready"), sem("pass2_soft_ready"))
        p2.gate_ready, p2.same_ready, p2.msg_t_ready = (
            sem("pass2_gate_ready"), sem("pass2_same_ready"), sem("pass2_msg_t_ready"))
        p2.turned, p2.msg_ready = sem("pass2_turned"), sem("pass2_msg_ready")
        p2.merged, p2.drow_ready = sem("pass2_merged"), sem("pass2_drow_ready")
        p2.drow_free = sem("pass2_drow_free")
        p2.z_in, p2.scattered = ring("pass2_z_in", SL), ring("pass2_scattered", ACCS)
        fin_in, fin_out, fin_step = ring("fin_in", 3), ring("fin_out", 3), sem("fin_step")

        def stepper(eng, s, base=0):
            n = [0]

            def step(ins):
                n[0] += 1
                ins.then_inc(s, 1)
                eng.wait_ge(s, base + n[0])
            step.n = n
            return step

        def windows(eng, g):
            word = nc.values_load(words[0:1, ds(g, 1)], engines=(eng.engine,), min_val=0,
                                  max_val=64 * (NT - 1) + NT - 1,
                                  skip_runtime_bounds_check_because="dst lies in the padded nodes")
            return eng.snap(word // 64), eng.snap(word % 64 + 1)

        def window(w):
            return nc.s_assert_within(w, 0, NT - 1,
                                      skip_runtime_bounds_check_because="dst lies in the padded nodes")

        def tick(eng, reg):
            eng.reg_add(reg, reg, 1)
            return eng.snap(reg, min_val=1, max_val=NG * NT)

        def in_turn(eng, lag, body):
            for s in range(SL):
                body(0, s)
            with eng.Fori(1, ITER) as i:
                for s in range(SL):
                    body(i, s)
            for s in range(lag):
                body(ITER, s)

        def back(i, s, n):
            i, s = (i, s - n) if s >= n else (i - 1, s - n + SL)
            if isinstance(i, int) and not 0 <= i < ITER:
                return None
            return i, s

        def rows_of(tab, i):
            return tab[ds(i * (NB * P), NB * P), :].rearrange("(j p) f -> p j f", p=P)

        def runs_of(tab, i):
            return tab[i * (NB * P):(i + 1) * (NB * P), :].rearrange("(p j) f -> p (j f)", j=NB)

        def row16(tab, g):
            return tab[ds(g, 1), :].to_broadcast([P, GE])

        def square(tab, g):
            return tab[ds(g, 1)].rearrange("a p e -> (a p) e")

        def node_tiles(t, i):
            return t[:, i * NB:(i + 1) * NB, :].rearrange("p a b -> p (a b)")

        def as_tiles(ap):
            return ap.rearrange("p (a b) -> p a b", b=F)

        def part(i, j):
            return parts[:, i % 5, :].rearrange("p (a b) -> p a b", b=F3)[:, :, j * F:(j + 1) * F]

        def pq_tiles(c):
            j0, j1 = SUBS[c % len(SUBS)]
            return c // len(SUBS) * NB + j0, j1 - j0

        def pq_bank(c, half):
            b = 2 + 3 * (c % 2)
            return PS[:, b:b + pq_tiles(c)[1], half * H2:(half + 1) * H2]

        def q_part(c, j):
            t, n = pq_tiles(c)
            return Q[:, j, t:t + n, :]

        def q_rest(c):
            return qr[:, c % 2, 0:pq_tiles(c)[1] * H2].rearrange("p (a b) -> p a b", b=H2)

        def all_stored(eng, ring):
            for q in range(len(ring)):
                eng.wait_ge(ring[q], 16 * len(range(q, NI, len(ring))))

        block = ctx.enter_context(nc.Block())

        @block.sync
        def _(sp):
            for i in range(NI):
                sp.dma_start(X[:, i * NB:(i + 1) * NB, :], rows_of(x, i)).then_inc(in_x[i], 16)
            sp.dma_start(dr_i[0:HALF], dst_rows.rearrange("(p c) e -> p c e", c=2)).then_inc(in_idx, 16)
            sp.dma_start(sr_i[0:HALF], src_rows.rearrange("(p c) e -> p c e", c=2)).then_inc(in_idx, 16)
            sp.dma_start(dst_i, dst_cols).then_inc(in_idx, 16)
            sp.dma_start(src_i[:], src_cols).then_inc(in_idx, 16)
            for t, d in ((W1N, w1n), (W1R, w1r), (W2N, w2n), (W2R, w2r), (WC, wc), (WAB, wab),
                         (B1, b1.to_broadcast([P, F])), (B2, b2.to_broadcast([P, F])),
                         (LB, lb), (GB, gamma_beta)):
                sp.dma_start(t[:], d).then_inc(in_w, 16)

            def zero_rows(i):
                for k in range(2, ACCS):
                    sp.dma_start(acc_tab[k][ds(i * P, P), :], zero).then_inc(acc_zeroed, 16)

            def store_parts(k, tab):
                for i in range(NI):
                    sp.wait_ge(k.part[2], i + 1)
                    sp.dma_start(rows_of(tab, i), parts[:, i % 5, :].rearrange("p (j f) -> p j f", f=F3)
                                 ).then_inc(k.stored[i % 5], 16)

            def load_src(c):
                with sp.Fori(0, ITER) as i:
                    for j in range(2):
                        sp.wait_ge(conv[c].counted, i * (2 * GT) + (j + 1) * GT)
                        sp.dma_start(s16[:, j, :], row16(src16_tab, i * SL + 2 * j + c)
                                     ).then_inc(conv[c].s16_landed[j], 16)
                    if c == 0:
                        zero_rows(i)

            store_parts(ln, h_tab[0])
            sp.wait_ge(natural_ready, 3)
            sp.dma_start(dst16_tab.rearrange("(p c) e -> p c e", c=2), dr16[0:HALF]).then_inc(natural_stored, 16)
            sp.dma_start(src16_tab.rearrange("(p c) e -> p c e", c=2), sr16[0:HALF]).then_inc(natural_stored, 16)
            sp.dma_start(win_tab.rearrange("(p c) -> p c", c=2), gw_i[0:HALF]).then_inc(natural_stored, 16)
            sp.wait_ge(natural_stored, 48)
            sp.dma_start(words[:], win_tab.rearrange("(a g) -> a g", a=1)).then_inc(words_in, 16)
            sp.wait_ge(zero_ready, 1)
            for k in range(ACCS):
                sp.dma_start(acc_tab[k][NP:NP + P, :], zero).then_inc(acc_zeroed, 16)
            load_src(0)
            store_parts(node[0], h_tab[1])
            load_src(1)
            for i in range(NI):
                sp.wait_ge(node[1].x_ready, i + 1)
                sp.dma_start(rows_of(acc_tab[0], i), X[:, i * NB:(i + 1) * NB, :]).then_inc(node[1].stored, 16)
            for i in range(NI + 1):
                if i < NI:
                    sp.wait_ge(node[1].h_ready, i + 1)
                    sp.dma_start(rows_of(acc_tab[1], i), H[:, i * NB:(i + 1) * NB, :]).then_inc(node[1].stored, 16)
                if i >= 1:
                    sp.wait_ge(pq.p_ready, len(SUBS) * i)
                    sp.dma_start(rows_of(p_tab, i - 1), p_s[:, (i - 1) % 2, :].rearrange("p (j f) -> p j f", f=H2)
                                 ).then_inc(pq.p_stored[(i - 1) % 2], 16)

            def load_edges(g, s):
                sp.dma_start(ebuf[:, s, :], square(edge_t, g)).then_inc(p1.edges_landed[s], 16)
                sp.dma_start(d16[:, s, :], row16(dst16_tab, g)).then_inc(p1.edges_landed[s], 16)

            all_stored(sp, pq.p_stored)
            sp.wait_ge(pq.part[2], CH)
            sp.sem_inc(p1.z_free, 2)
            for s in range(SL):
                load_edges(s, s)

            def edges_in_z_out(i, s):
                g, q, n = i * SL + s, s % 2, i * 2 + s // 2
                if not (isinstance(i, int) and i == ITER - 1):
                    sp.wait_ge(p1.done, g + SL + 1)
                    load_edges(g + SL, s)
                if back(i, s, 2):
                    sp.wait_ge(p1.z_stored[q], n * 16)
                    sp.sem_inc(p1.z_free, 1)
                sp.wait_ge(p1.z_ready, g + 3)
                sp.dma_start(square(z_tab, g), zb[:, q, :]).then_inc(p1.z_stored[q], 16)
            for s in range(SL):
                edges_in_z_out(0, s)
            with sp.Fori(1, ITER - 1) as i:
                for s in range(SL):
                    edges_in_z_out(i, s)
            for s in range(SL):
                edges_in_z_out(ITER - 1, s)
            for q in range(2):
                sp.wait_ge(p1.z_stored[q], 16 * (NG // 2))

            sp.wait_ge(p1.done, NG + SL)
            with sp.Fori(0, ITER) as i:
                for s in range(SL):
                    g = i * SL + s
                    sp.wait_ge(p2.soft_ready, g + 1)
                    sp.wait_ge(p2.same_ready, g + 1)
                    sp.dma_start(zin[:, s, :], square(z_tab, g)).then_inc(p2.z_in[s], 16)
                    sp.dma_start(s16b[:, s, :], row16(src16_tab, g)).then_inc(p2.z_in[s], 16)

            def store_out(i):
                q = i % 3
                sp.wait_ge(fin_step, (ACCS - 1) * (i + 1))
                sp.dma_start(runs_of(out, i), fin[:, q, 0:NB * F]).then_inc(fin_out[q], 16)
            for k in range(ACCS):
                sp.wait_ge(p2.scattered[k], 16 * ITER * ACC_OF.count(k))
            for i in range(NI):
                q = i % 3
                if i >= 3:
                    sp.wait_ge(fin_out[q], 16 * (i // 3))
                for k in range(ACCS):
                    sp.dma_start(fin[:, q, k * NB * F:(k + 1) * NB * F], runs_of(acc_tab[k], i)).then_inc(fin_in[q], 16)
                if i >= 1:
                    store_out(i - 1)
            store_out(NI - 1)
            all_stored(sp, fin_out)

        @block.gpsimd
        def _(pool):
            nc.gpsimd.iota(iota_i[:], pattern=[[1, F]], base=0, channel_multiplier=0).then_inc(iota_done, 1)
            nc.gpsimd.iota(win_i[:, 0, :], pattern=[[-P, NT]], base=0, channel_multiplier=0).then_inc(iota_done, 1)
            nc.gpsimd.iota(win_i[:, 1, :], pattern=[[P, NT]], base=0, channel_multiplier=1).then_inc(iota_done, 1)

            nc.gpsimd.memset(zero, 0.0).then_inc(zero_ready, 1)
            nc.gpsimd.memset(ones[:], 1.0)
            nc.gpsimd.memset(ones_bf[:], 1.0)
            nc.gpsimd.memset(AGG, 0.0).then_inc(agg_zeroed, 1)

            def gather_all(n, table, buf, width):
                with pool.Fori(0, ITER) as i:
                    for s in range(SL):
                        pool.wait_ge(idx_ready[s], i + (n * ITER + 1))
                        pool.sem_inc(wait_done, 1)
                        for t in range(s * GT, s * GT + GT):
                            nc.gpsimd.indirect_dma_start(buf[:, t, 0:width], None, table,
                                                         bass.IndirectOffsetOnAxis(idx_slot[:, t:t + 1], 0)
                                                         ).then_inc(rows_landed[s], 16)

            all_stored(pool, ln.stored)
            gather_all(0, h_tab[0], rows, F3)
            pool.wait_ge(node[0].part[0], NI)
            nc.gpsimd.memset(AGG, 0.0).then_inc(agg_zeroed, 1)
            all_stored(pool, node[0].stored)
            gather_all(1, h_tab[1], rows, F3)
            all_stored(pool, pq.p_stored)
            gather_all(2, p_tab, prow, H2)

            def scatter(i, s):
                g = i * SL + s
                pool.wait_ge(p2.drow_ready, g + 3)
                if s == 1 and not isinstance(i, int):
                    pool.wait_ge(p2.scattered[ACCS - 1], i * 16)
                for k in range(GT):
                    n = s * GT + k
                    acc = ACC_OF[n]
                    before = ACC_OF[:n].count(acc)
                    if not isinstance(i, int) or before:
                        pool.wait_ge(p2.scattered[acc], (i * ACC_OF.count(acc) + before) * 16)
                    pool.sem_inc(p2.drow_free if k == GT - 1 else wait_done, 1)
                    nc.gpsimd.indirect_dma_start(acc_tab[acc], bass.IndirectOffsetOnAxis(idx_slot[:, n:n + 1], 0),
                                                 drow[:, s, k * F:(k + 1) * F], None,
                                                 compute_op=ALU.add).then_inc(p2.scattered[acc], 16)
            pool.wait_ge(node[1].stored, 16 * 2 * NI)
            pool.sem_inc(p2.drow_free, SL - 2)
            for s in range(SL):
                scatter(0, s)
            with pool.Fori(1, ITER) as i:
                for s in range(SL):
                    scatter(i, s)

        @block.scalar
        def _(act):
            def put_idx(table, g, s, signal):
                return nc.scalar.copy(idx_slot[:, s * GT:(s + 1) * GT], table[:, ds(g * GT, GT)]).then_inc(signal, 1)

            def squares(k):
                for i in range(NI):
                    act.wait_ge(k.centred, i + 1)
                    if i >= 2:
                        act.wait_ge(k.squares_used, i - 1)
                    nc.scalar.activation(o_s[:, i % 2, :], node_tiles(H, i), ACT.Square).then_inc(k.squared, 1)
                act.wait_ge(k.var, 1)
                nc.scalar.activation(stat[:, 3, :], stat[:, 2, :], ACT.Sqrt).then_inc(k.root, 1)

            def split(k, relu_of=None):
                for i in range(NI + 2):
                    if i < NI:
                        act.wait_ge(k.source, i + 1)
                        if i >= 5:
                            act.wait_ge(k.stored[i % 5], 16 * (i // 5))
                        out = part(i, 0)
                        if relu_of is None:
                            nc.scalar.copy(out, as_tiles(node_tiles(H, i))).then_inc(k.part[0], 1)
                        else:
                            nc.scalar.activation(node_tiles(H, i), relu_of[:, i % 2, :], ACT.Relu)
                            nc.scalar.activation(out, as_tiles(relu_of[:, i % 2, :]), ACT.Relu).then_inc(k.part[0], 1)
                    for j in (1, 2):
                        if 0 <= i - j < NI:
                            act.wait_ge(k.rest[j - 1], i - j + 1)
                            nc.scalar.copy(part(i - j, j), as_tiles(rest[:, (i - j) % 3, :])).then_inc(k.part[j], 1)

            squares(ln)
            split(ln)

            for c in range(2):
                k, n = conv[c], node[c]
                if c == 0:
                    act.wait_ge(in_idx, 64)
                for s in range(SL):
                    put_idx(src_i, s, s, idx_ready[s])
                if c == 0:
                    nc.scalar.copy(dr16[0:HALF], dr_i[0:HALF]).then_inc(natural_ready, 1)
                    nc.scalar.copy(sr16[0:HALF], sr_i[0:HALF]).then_inc(natural_ready, 1)
                    nc.scalar.copy(src_f[:], src_i[:])
                    nc.scalar.copy(dst_f[:], dst_i).then_inc(floats_ready, 1)

                def conv_step(i, last=False):
                    for s in range(SL):
                        if s == 0:
                            act.sem_inc(wait_done, 1)
                            act.wait_ge(n.root_turned, i + 1)
                            act.sem_inc(wait_done, 1)
                            nc.scalar.copy(hs, H[:, ds(i, 1), :].rearrange("p a f -> p (a f)")
                                           ).then_inc(n.root_staged, 1)
                        act.wait_ge(k.group_done, i * SL + s + 1)
                        if not last:
                            put_idx(src_i, (i + 1) * SL + s, s, idx_ready[s])
                        if s == 1:
                            act.wait_ge(n.root_turned, i + 2)
                            nc.scalar.copy(hst, PS[:, 2, 0:F]).then_inc(n.root_lhs, 1)
                        elif s == 3:
                            act.wait_ge(n.root_product, i + 1)
                            act.sem_inc(wait_done, 1)
                            nc.scalar.copy((H if c == 0 else X)[:, ds(i, 1), :].rearrange("p a f -> p (a f)"),
                                           PS[:, 3, 0:F]).then_inc(n.root_done, 1)
                with act.Fori(0, ITER - 1) as i:
                    conv_step(i)
                conv_step(ITER - 1, last=True)
                if c == 0:
                    split(n, relu_of=o_s)
                else:
                    squares(n)

            def turned_h(i):
                act.wait_ge(pq.turned, i + 1)
                if i >= 2:
                    act.wait_ge(pq.product, len(SUBS) * (i - 1))
                nc.scalar.copy(ht[:, i % 2, :], banks(0)).then_inc(pq.evicted, 1)

            def second_part(c):
                act.wait_ge(pq.rest[0], c + 1)
                nc.scalar.copy(q_part(c, 1), q_rest(c)).then_inc(pq.part[1], 1)

            turned_h(0)
            for c in range(CH):
                i, (j0, j1) = c // len(SUBS), SUBS[c % len(SUBS)]
                act.wait_ge(pq.product, c + 1)
                if i >= 2 and j0 == 0:
                    act.wait_ge(pq.p_stored[i % 2], 16 * (i // 2))
                nc.scalar.copy(p_s[:, i % 2, j0 * H2:j1 * H2].rearrange("p (j f) -> p j f", f=H2), pq_bank(c, 0)
                               ).then_inc(pq.p_ready, 1)
                nc.scalar.copy(q_part(c, 0), pq_bank(c, 1)).then_inc(pq.part[0], 1)
                if j0 == 0 and i + 1 < NI:
                    turned_h(i + 1)
                if c >= 1:
                    second_part(c - 1)
            second_part(CH - 1)

            def evict(g, q):
                act.wait_ge(p1.done, g + SL + 1)
                act.wait_ge(p1.z_ready, g + 1)
                for h in range(2):
                    ins = nc.scalar.activation(zt[:, q, h * GE:(h + 1) * GE], PS[:, 2 * q + h, :], ACT.Identity,
                                               bias=LB[:, h:h + 1])
                ins.then_inc(p1.evicted, 1)
            all_stored(act, pq.p_stored)
            act.wait_ge(pq.part[2], CH)
            act.sem_inc(p1.evicted, 2)
            for s in range(SL):
                put_idx(src_i, s, s, idx_ready[s])
            with act.Fori(0, ITER - 1) as i:
                for s in range(SL):
                    g = i * SL + s
                    evict(g, s % 2)
                    put_idx(src_i, g + SL, s, idx_ready[s])
            for s in range(SL):
                evict(NG - SL + s, s % 2)

            act.wait_ge(norm.var, 1)
            nc.scalar.activation(bn[:, 6:8], bn[:, 4:6], ACT.Sqrt).then_inc(norm.root, 1)

            def softened(i, s):
                g = i * SL + s
                act.wait_ge(p2.abs_ready, g + 1)
                nc.scalar.activation(soft[:, s, :], soft[:, s, :], ACT.Exp, scale=-1.0).then_inc(p2.act_step, 1)
                act.wait_ge(p2.act_step, g + 1)
                nc.scalar.activation(soft[:, s, :], soft[:, s, :], ACT.Ln, bias=1.0).then_inc(p2.ln_ready, 1)

            def gate(i, s):
                g = i * SL + s
                act.wait_ge(p2.soft_ready, g + SL + 1)
                nc.scalar.activation(soft[:, s, 0:GE], soft[:, s, 0:GE], ACT.Exp, scale=-1.0
                                     ).then_inc(p2.gate_ready, 1)

            def take_msg(i, s):
                g, q = i * SL + s, s % 2
                act.wait_ge(p2.turned, g + 3)
                act.wait_ge(p2.merged, g + 1)
                nc.scalar.copy(msg[:, q, :], PS[:, 2 + q, :]).then_inc(p2.msg_ready, 1)

            def take_sums(i, s):
                g = i * SL + s
                act.wait_ge(p2.merged, g + 3)
                act.wait_ge(p2.drow_free, g + 1)
                nc.scalar.copy(drow[:, s, :], PS[:, 4 + s % 2, :])
                put_idx(scat_i, g, s, p2.drow_ready)

            def pass2(i, s):
                for n, stage in ((0, softened), (1, gate), (3, take_msg), (4, take_sums)):
                    at = back(i, s, n)
                    if at:
                        stage(*at)

            nc.scalar.preload_act_table_set("natural_log_exp_and_others")
            act.wait_ge(norm.ready, 1)
            act.sem_inc(p2.msg_ready, 2)
            act.sem_inc(p2.drow_ready, 2)
            in_turn(act, 4, pass2)

        @block.vector
        def _(dve):
            v = nc.vector
            step = stepper(dve, chain)
            dve.wait_ge(iota_done, 3)
            step(v.tensor_copy(iota[:], iota_i[:]))
            step(v.tensor_copy(wneg[:], win_i[:, 0, :]))
            step(v.tensor_copy(wpos[:], win_i[:, 1, :]))
            step(v.tensor_scalar(ident[:], iota[:], wpos[:, 0:1], None, ALU.is_equal))
            v.tensor_scalar(lower[:], iota[:], wpos[:, 0:1], None, ALU.is_lt).then_inc(consts, 1)

            def split(k, combine=None):
                for i in range(NI + 2):
                    if combine and i < NI:
                        combine(i)
                    for j in (0, 1):
                        n = i - j - (1 if combine else 0)
                        if not 0 <= n < NI:
                            continue
                        dve.wait_ge(k.part[j], n + 1)
                        if j == 0 and n >= 3:
                            dve.wait_ge(k.part[2], n - 2)
                        if j == 1:
                            dve.wait_ge(k.rest[0], n + 1)
                        v.tensor_tensor(as_tiles(rest[:, n % 3, :]),
                                        as_tiles(rest[:, n % 3, :] if j else node_tiles(H, n)), part(n, j),
                                        ALU.subtract).then_inc(k.rest[j], 1)

            def inverse_root(step, var, root, inv, tmp):
                step(v.reciprocal(inv, root))
                step(v.tensor_tensor(tmp, inv, inv, ALU.mult))
                step(v.tensor_tensor(tmp, tmp, var, ALU.mult))
                step(v.tensor_scalar(tmp, tmp, -0.5, 1.5, ALU.mult, ALU.add))
                step(v.tensor_tensor(inv, inv, tmp, ALU.mult))

            def row_sum(i):
                return v.tensor_reduce(stat[:, 0, i * NB:(i + 1) * NB], X[:, i * NB:(i + 1) * NB, :], AX.X, ALU.add)

            def layer_norm(k, out_ready):
                step(v.tensor_scalar(stat[:, 1, :], stat[:, 0, :], -1.0 / F, None, ALU.mult))
                for i in range(NI + 1):
                    if i < NI:
                        t = slice(i * NB, (i + 1) * NB)
                        v.tensor_tensor(H[:, t, :], X[:, t, :], bc(stat[:, 1, t], F), ALU.add).then_inc(k.centred, 1)
                    if i >= 1:
                        dve.wait_ge(k.squared, i)
                        v.tensor_reduce(stat[:, 0, (i - 1) * NB:i * NB], as_tiles(o_s[:, (i - 1) % 2, :]), AX.X, ALU.add
                                        ).then_inc(k.squares_used, 1)
                dve.wait_ge(k.squares_used, NI)
                v.tensor_scalar(stat[:, 2, :], stat[:, 0, :], 1.0 / F, EPS, ALU.mult, ALU.add).then_inc(k.var, 1)
                dve.wait_ge(k.root, 1)
                inverse_root(step, stat[:, 2, :], stat[:, 3, :], stat[:, 4, :], stat[:, 5, :])
                for i in range(NI):
                    t = slice(i * NB, (i + 1) * NB)
                    v.scalar_tensor_tensor(H[:, t, :], H[:, t, :], 0.0, bc(stat[:, 4, t], F), ALU.max, ALU.mult
                                           ).then_inc(out_ready, 1)
                    yield i

            for i in range(NI):
                dve.wait_ge(in_x[i], 16)
                step(row_sum(i))
            for i in layer_norm(ln, ln.source):
                pass
            split(ln)

            dve.wait_ge(in_idx, 64)
            d = dr_i[0:HALF]
            step(v.tensor_reduce(gmn_i[0:HALF], d, AX.X, ALU.min))
            step(v.tensor_reduce(gmx_i[0:HALF], d, AX.X, ALU.max))
            step(v.tensor_scalar(gmn_i[0:HALF], gmn_i[0:HALF], 7, None, ALU.logical_shift_right))
            step(v.tensor_scalar(gmx_i[0:HALF], gmx_i[0:HALF], 7, None, ALU.logical_shift_right))
            v.scalar_tensor_tensor(gw_i[0:HALF], gmn_i[0:HALF], 64.0, gmx_i[0:HALF], ALU.mult, ALU.add
                                   ).then_inc(natural_ready, 1)

            def add_sums(k, n, w):
                dve.wait_ge(k.sum_ready, n)
                dve.wait_ge(k.sum_added, n)
                a = AGG[:, ds(w, 1), :].rearrange("p a b -> p (a b)")
                v.tensor_tensor(a, a, ps_agg, ALU.add).then_inc(k.sum_added, 1)

            def sum_by_window(k, g, pair, before):
                lo, hi = windows(dve, g)
                with dve.Fori(lo, hi) as w:
                    n, w = tick(dve, pair), window(w)
                    v.scalar_tensor_tensor(onehot[:, ds(n % 2, 1), :].rearrange("p a (t b) -> p (a t) b", b=P),
                                           bc(dst_f[:, ds(g * GT, GT)], P), wneg[:, ds(w, 1)],
                                           rep(iota[:], GT), ALU.add, ALU.is_equal).then_inc(k.onehot_ready, 1)
                    add_sums(k, n, dve.snap(before, min_val=0, max_val=NT - 1))
                    dve.reg_mov(before, w)

            def count_repeats(k, g, j, i):
                dve.wait_ge(k.s16_landed[j], i * 16 + 16)
                for t in range(GT):
                    dve.wait_ge(k.counted, i * (2 * GT) + j * GT + t + 2 * GT - 1)
                    v.scalar_tensor_tensor(junk[:, t % 2, :], s16[:, j, t * P:(t + 1) * P],
                                           src_f[:, ds(g * GT + t, 1)], lower[:], ALU.is_equal, ALU.mult,
                                           accum_out=cnt[:, ds(g * GT + t, 1)]).then_inc(k.counted, 1)

            dve.wait_ge(natural_stored, 48)
            dve.wait_ge(words_in, 16)
            dve.wait_ge(floats_ready, 1)
            for c in range(2):
                k, n = conv[c], node[c]
                dve.wait_ge(agg_zeroed, c + 1)
                dve.sem_inc(k.sum_added, 1)
                pair, before = dve.alloc_register(f"dve_pair{c}"), dve.alloc_register(f"dve_before{c}")
                dve.reg_mov(pair, 0)
                dve.reg_mov(before, 0)
                v.memset(ps_agg, 0.0).then_inc(k.sum_ready, 1)
                dve.sem_inc(k.counted, 2 * GT)
                with dve.Fori(0, ITER) as i:
                    for s in range(SL):
                        sum_by_window(k, i * SL + s, pair, before)
                        if s % 2 == c:
                            count_repeats(k, i * SL + s, s // 2, i)
                add_sums(k, tick(dve, pair), dve.snap(before, min_val=0, max_val=NT - 1))
                dve.wait_ge(k.sum_added, tick(dve, pair))
                if c == 1:
                    dve.wait_ge(k.counted, (NG // 2 + 2) * GT)
                    big, _ = carve(q_space, 0, TILES)
                    step(v.tensor_scalar(bn[:, 0:1], wpos[:, 0:1], float(NP), None, ALU.add))
                    step(v.tensor_scalar(big, src_f[:], -1.0, bn[:, 0:1], ALU.mult, ALU.add))
                    step(v.tensor_scalar(cnt[:], cnt[:], 0.0, None, ALU.is_gt))
                    step(v.tensor_tensor(big, big, cnt[:], ALU.mult))
                    step(v.tensor_tensor(scat_i[:], big, src_f[:], ALU.add))
                dve.wait_ge(n.root_done, NT)
                if c == 0:
                    deg = AGG[:, :, F:F + 1].rearrange("p a b -> p (a b)")
                    step(v.tensor_scalar(stat[:, 0, :], deg, 1.0, None, ALU.max))
                    step(v.reciprocal(inv_deg[:], stat[:, 0, :]))

                def combine(i):
                    t = slice(i * NB, (i + 1) * NB)
                    dve.wait_ge(n.product, i + 1)
                    if c == 0 and i >= 2:
                        dve.wait_ge(n.part[0], i - 1)
                    o = as_tiles(o_s[:, i % 2, :])
                    step(v.tensor_tensor(o, as_tiles(banks(4 + i % 2 * 2)), bc(inv_deg[:, t], F), ALU.mult))
                    if c == 0:
                        v.tensor_tensor(o, o, H[:, t, :], ALU.add).then_inc(n.source, 1)
                    else:
                        v.tensor_tensor(X[:, t, :], o, X[:, t, :], ALU.add).then_inc(n.x_ready, 1)
                        dve.wait_ge(n.x_ready, i + 1)
                        step(row_sum(i))

                if c == 0:
                    split(n, combine)

            for i in range(NI):
                combine(i)

            def rests(c):
                if c < CH:
                    dve.wait_ge(pq.part[0], c + 1)
                    if c >= 2:
                        dve.wait_ge(pq.part[2], c - 1)
                    v.tensor_tensor(q_rest(c), pq_bank(c, 1), q_part(c, 0), ALU.subtract).then_inc(pq.rest[0], 1)
                if c >= 1:
                    dve.wait_ge(pq.part[1], c)
                    dve.wait_ge(pq.rest[0], c)
                    v.tensor_tensor(q_rest(c - 1), q_rest(c - 1), q_part(c - 1, 1), ALU.subtract
                                    ).then_inc(pq.rest[1], 1)
                    dve.wait_ge(pq.rest[1], c)
                    v.tensor_copy(q_part(c - 1, 2), q_rest(c - 1)).then_inc(pq.part[2], 1)

            for i in layer_norm(node[1], node[1].h_ready):
                if i >= 2:
                    for c in range(len(SUBS)):
                        rests((i - 2) * len(SUBS) + c)
            for c in range(len(SUBS) * (NI - 2), CH + 1):
                rests(c)

            def onehot_by_window(i, s, pair):
                lo, hi = windows(dve, i * SL + s)
                dve.wait_ge(p1.edges_landed[s], i * 32 + 32)
                with dve.Fori(lo, hi) as w:
                    m, w = tick(dve, pair), window(w)
                    dve.wait_ge(p1.oht_used, m)
                    v.tensor_scalar(oht[:, ds(m % 2, 1), :].rearrange("p a e -> p (a e)"), d16[:, s, :],
                                    wpos[:, ds(w, 1)], None, ALU.is_equal).then_inc(p1.oht_ready, 1)

            def finish_z(g, q, valid=GE):
                dve.wait_ge(p1.evicted, g + 3)
                dve.wait_ge(p1.z_free, g + 1)
                dve.wait_ge(p1.stats_done, g + 1)
                v.tensor_tensor(zb[:, q, :], zt[:, q, :], PS[:, 4 + 2 * q:6 + 2 * q, :].rearrange("p a b -> p (a b)"),
                                ALU.add).then_inc(p1.z_ready, 1)
                dve.wait_ge(p1.z_ready, g + 3)
                for h in range(2):
                    ins = v.bn_stats(stats[:, h, ds(g, 1), :].rearrange("p a b -> p (a b)"),
                                     zb[:, q, h * GE:h * GE + valid])
                ins.then_inc(p1.stats_done, 1)

            dve.wait_ge(pq.part[2], CH)
            all_stored(dve, pq.p_stored)
            dve.sem_inc(p1.z_ready, 2)
            dve.sem_inc(p1.stats_done, 2)
            pair = dve.alloc_register("dve_pair2")
            dve.reg_mov(pair, 0)

            def pass1(i, s):
                if back(i, s, 0):
                    onehot_by_window(i, s, pair)
                at = back(i, s, 1)
                if at:
                    g = at[0] * SL + at[1]
                    finish_z(g, at[1] % 2, E - g * GE if isinstance(g, int) and g == NG - 1 else GE)
            in_turn(dve, 1, pass1)
            dve.wait_ge(p1.stats_done, NG + 2)

            nst = stepper(dve, norm.step)
            for h in range(2):
                nst(v.bn_aggr(bn[:, 2 * h:2 * h + 2], stats[:, h].rearrange("p a b -> p (a b)")))
            mv = bn[:, 0:4].rearrange("p (h k) -> p k h", k=2)
            v.tensor_scalar(bn[:, 4:6], mv[:, 1, :], EPS, None, ALU.add).then_inc(norm.var, 1)
            dve.wait_ge(norm.root, 1)
            inverse_root(nst, bn[:, 4:6], bn[:, 6:8], bn[:, 14:16], bn[:, 16:18])
            nst(v.tensor_tensor(bn[:, 8:10], bn[:, 14:16], GB[:, 0:2], ALU.mult))
            nst(v.tensor_tensor(bn[:, 18:20], mv[:, 0, :], bn[:, 8:10], ALU.mult))
            nst(v.tensor_tensor(bn[:, 10:12], GB[:, 2:4], bn[:, 18:20], ALU.subtract))
            nst(v.tensor_scalar(bn[:, 12:13], bn[:, 8:9], -1.0, None, ALU.mult))
            v.tensor_scalar(bn[:, 13:14], bn[:, 10:11], -1.0, None, ALU.mult).then_inc(norm.ready, 1)

            def take_z(i, s):
                g = i * SL + s
                dve.wait_ge(p2.z_in[s], i * 32 + 32)
                v.tensor_scalar(zin[:, s, 0:GE], zin[:, s, 0:GE], bn[:, 12:13], bn[:, 13:14], ALU.mult, ALU.add
                                ).then_inc(p2.dve_step, 1)
                v.tensor_scalar(zin[:, s, GE:2 * GE], zin[:, s, GE:2 * GE], bn[:, 9:10], bn[:, 11:12],
                                ALU.mult, ALU.add).then_inc(p2.dve_step, 1)
                dve.wait_ge(p2.dve_step, g * 2 + 2)
                v.tensor_scalar(soft[:, s, :].bitcast(I32), zin[:, s, :].bitcast(I32), 0x7FFFFFFF, None,
                                ALU.bitwise_and).then_inc(p2.abs_ready, 1)

            def soften(i, s):
                g = i * SL + s
                dve.wait_ge(p2.ln_ready, g + 1)
                v.scalar_tensor_tensor(soft[:, s, :], zin[:, s, :], 0.0, soft[:, s, :], ALU.max, ALU.add
                                       ).then_inc(p2.soft_ready, 1)

            def message(i, s):
                g, q = i * SL + s, s % 2
                dve.wait_ge(p2.merged, g + 1)
                v.tensor_tensor(same[:, q, :].rearrange("p (a b) -> p a b", b=P),
                                s16b[:, s, :].rearrange("p (a b) -> p a b", b=P),
                                bc(src_f[:, ds(g * GT, GT)], P), ALU.is_equal).then_inc(p2.same_ready, 1)
                dve.wait_ge(p2.gate_ready, g + 1)
                dve.wait_ge(p2.turned, g + 1)
                v.tensor_tensor(msg_t[:, q, :], soft[:, s, 0:GE], soft[:, s, GE:2 * GE], ALU.mult
                                ).then_inc(p2.msg_t_ready, 1)

            def pass2(i, s):
                for n, stage in ((0, take_z), (1, soften), (2, message)):
                    at = back(i, s, n)
                    if at:
                        stage(*at)

            dve.wait_ge(norm.ready, 1)
            dve.sem_inc(p2.soft_ready, SL)
            dve.sem_inc(p2.same_ready, SL)
            dve.sem_inc(p2.msg_t_ready, 2)
            in_turn(dve, 2, pass2)

            for i in range(NI):
                q = i % 3
                st = stepper(dve, fin_step, (ACCS - 1) * i)
                dve.wait_ge(fin_in[q], 16 * ACCS * (i // 3 + 1))
                total = fin[:, q, 0:NB * F]
                for k in range(1, ACCS):
                    st(v.tensor_tensor(total, total, fin[:, q, k * NB * F:(k + 1) * NB * F], ALU.add))

        @block.tensor
        def _(pe):
            mm, turn = nc.tensor.matmul, nc.tensor.transpose
            pe.wait_ge(consts, 1)
            pe.wait_ge(agg_zeroed, 1)
            pe.wait_ge(in_w, 160)
            pe.wait_ge(words_in, 16)

            def place(b, j):
                return PS[:, b + j // 4, (j % 4) * F:(j % 4 + 1) * F]

            for c in range(2):
                k, n = conv[c], node[c]
                pair = pe.alloc_register(f"pe_pair{c}")
                pe.reg_mov(pair, 0)
                wn, wr, b = (W1N, W1R, B1) if c == 0 else (W2N, W2R, B2)
                pe.sem_inc(n.root_turned, 1)
                with pe.Fori(0, ITER) as i:
                    for s in range(SL):
                        lo, hi = windows(pe, i * SL + s)
                        pe.wait_ge(rows_landed[s], i * (16 * GT) + 16 * GT * (c * ITER + 1))
                        with pe.Fori(lo, hi):
                            m = tick(pe, pair)
                            pe.wait_ge(k.onehot_ready, m)
                            pe.wait_ge(k.sum_added, m + 1)
                            hot = onehot[:, ds(m % 2, 1), :].rearrange("p a e -> p (a e)")
                            for t in range(GT):
                                for j in (2, 1, 0):
                                    ins = mm(ps_agg[:, 0:F], rows[:, s * GT + t, j * F:(j + 1) * F],
                                             hot[:, t * P:(t + 1) * P],
                                             start=t == 0 and j == 2, stop=t == GT - 1 and j == 0,
                                             skip_group_check=True)
                            for t in range(GT):
                                ins = mm(ps_agg[:, F:F + 1], hot[:, t * P:(t + 1) * P], ones_bf[:, 0:1], start=t == 0,
                                         stop=t == GT - 1, skip_group_check=True)
                            ins.then_inc(k.sum_ready, 1)
                        pe.drain().then_inc(k.group_done, 1)
                        if s == 0:
                            pe.wait_ge(n.root_staged, i + 1)
                            turn(PS[:, 2, 0:F], hs, ident[:]).then_inc(n.root_turned, 1)
                        elif s == 2:
                            pe.wait_ge(n.root_lhs, i + 1)
                            mm(PS[:, 3, 0:F], hst, wr[:], start=True, stop=False)
                            ins = mm(PS[:, 3, 0:F], ones[0:1, :], b[0:1, :], start=False, stop=c == 0)
                            if c == 1:
                                ins = mm(PS[:, 3, 0:F], ident[:], X[:, ds(i, 1), :].rearrange("p a f -> p (a f)"),
                                         start=False, stop=True)
                            ins.then_inc(n.root_product, 1)
                tick(pe, pair)
                pe.wait_ge(k.sum_added, tick(pe, pair))
                for i in range(NI):
                    if i >= 2:
                        pe.wait_ge(node[0].source if c == 0 else node[1].x_ready, i - 1)
                    for j in range(NB):
                        ins = mm(place(4 + i % 2 * 2, j), AGG[:, i * NB + j, 0:F], wn[:], start=True, stop=True)
                    ins.then_inc(n.product, 1)

            def turn_h(i):
                pe.wait_ge(node[1].h_ready, i + 1)
                if i >= 1:
                    pe.wait_ge(pq.evicted, i)
                for j in range(NB):
                    ins = turn(place(0, j), H[:, i * NB + j, :], ident[:])
                ins.then_inc(pq.turned, 1)

            turn_h(0)
            for c in range(CH):
                i, (j0, j1) = c // len(SUBS), SUBS[c % len(SUBS)]
                if j0 == 0 and i + 1 < NI:
                    turn_h(i + 1)
                pe.wait_ge(pq.evicted, i + 1)
                if c >= 2:
                    pe.wait_ge(pq.rest[0], c - 1)
                for j in range(j0, j1):
                    bank = PS[:, 2 + 3 * (c % 2) + j - j0, :]
                    ins = mm(bank, ht[:, i % 2, j * F:(j + 1) * F], WAB[:], start=True, stop=True)
                ins.then_inc(pq.product, 1)

            pe.wait_ge(pq.part[2], CH)
            pe.sem_inc(p1.done, SL)
            pe.sem_inc(p1.oht_used, 2)
            pair = pe.alloc_register("pe_pair2")
            pe.reg_mov(pair, 0)
            with pe.Fori(0, ITER) as i:
                for s in range(SL):
                    g, q = i * SL + s, s % 2
                    lo, hi = windows(pe, g)
                    pe.wait_ge(p1.edges_landed[s], i * 32 + 32)
                    pe.wait_ge(p1.evicted, g + 1)
                    for h in range(2):
                        mm(PS[:, 2 * q + h, :], WC[:, h * F:(h + 1) * F], ebuf[:, s, :], start=True, stop=False,
                           skip_group_check=True)
                    with pe.Fori(lo, hi) as w:
                        m, w = tick(pe, pair), window(w)
                        pe.wait_ge(p1.oht_ready, m)
                        hot = oht[:, ds(m % 2, 1), :].rearrange("p a e -> p (a e)")
                        for h in range(2):
                            for j in range(3):
                                part = Q[:, j, ds(w, 1), h * F:(h + 1) * F].rearrange("p a b -> p (a b)")
                                ins = mm(PS[:, 2 * q + h, :], part, hot, start=False, stop=True,
                                         skip_group_check=True)
                        ins.then_inc(p1.oht_used, 1)
                    pe.wait_ge(rows_landed[s], i * (16 * GT) + 16 * GT * (2 * ITER + 1))
                    pe.wait_ge(p1.z_ready, g + 1)
                    for t in range(GT):
                        for h in range(2):
                            ins = turn(PS[:, 4 + 2 * q + h, t * P:(t + 1) * P],
                                       prow[:, s * GT + t, h * F:(h + 1) * F], ident[:])
                    ins.then_inc(p1.done, 1)

            def turn_msg(i, s):
                g, q = i * SL + s, s % 2
                pe.wait_ge(p2.msg_t_ready, g + 3)
                pe.wait_ge(p2.msg_ready, g + 1)
                for t in range(GT):
                    ins = turn(PS[:, 2 + q, t * P:(t + 1) * P], msg_t[:, q, t * P:(t + 1) * P], ident[:])
                ins.then_inc(p2.turned, 1)

            def merge(i, s):
                g, q = i * SL + s, s % 2
                pe.wait_ge(p2.msg_ready, g + 3)
                pe.wait_ge(p2.same_ready, g + SL + 1)
                pe.wait_ge(p2.drow_ready, g + 1)
                for t in range(GT):
                    c = slice(t * P, (t + 1) * P)
                    ins = mm(PS[:, 4 + q, c], same[:, q, c], msg[:, q, c], start=True, stop=True)
                ins.then_inc(p2.merged, 1)

            def pass2(i, s):
                for n, stage in ((0, turn_msg), (1, merge)):
                    at = back(i, s, n)
                    if at:
                        stage(*at)

            pe.wait_ge(norm.ready, 1)
            pe.sem_inc(p2.turned, 2)
            pe.sem_inc(p2.merged, 2)
            in_turn(pe, 1, pass2)


def kernel(x, src, dst, edge_attr_128, L0_gnn_W1_nbr, L0_gnn_W1_root, L0_gnn_b1, L0_gnn_W2_nbr,
           L0_gnn_W2_root, L0_gnn_b2, L1_gnn_W, L1_gnn_b, L1_gnn_gamma, L1_gnn_beta):
    import numpy as np
    import concourse.bacc as bacc
    from concourse import mybir
    from concourse.bass_utils import run_bass_kernel_spmd

    P, GE = 128, 512
    N, F = x.shape
    E = src.shape[0]
    NP = -(-N // P) * P
    NG = -(-E // GE)
    EP = NG * GE

    def c(a):
        return np.ascontiguousarray(np.asarray(a))

    def padded(a, n, fill):
        a = np.asarray(a)
        return np.concatenate([a, np.full((n - a.shape[0],) + a.shape[1:], fill, a.dtype)])

    sp, dp = padded(src, EP, N), padded(dst, EP, N)
    wt = np.asarray(L1_gnn_W).T
    arrays = {
        "x": padded(x, NP, 0),
        "src_cols": c(sp.reshape(EP // P, P).T), "dst_cols": c(dp.reshape(EP // P, P).T),
        "src_rows": sp.reshape(NG, GE), "dst_rows": dp.reshape(NG, GE),
        "edge_t": c(padded(edge_attr_128, EP, 0).reshape(NG, GE, F).transpose(0, 2, 1)),
        "w1n": c(L0_gnn_W1_nbr), "w1r": c(L0_gnn_W1_root), "w2n": c(L0_gnn_W2_nbr), "w2r": c(L0_gnn_W2_root),
        "b1": c(L0_gnn_b1).reshape(1, F), "b2": c(L0_gnn_b2).reshape(1, F),
        "wab": c(np.concatenate([wt[0:F], wt[F:2 * F]], axis=1)), "wc": c(wt[2 * F:3 * F]),
        "lb": c(np.asarray(L1_gnn_b).reshape(2, F).T),
        "gamma_beta": c(np.concatenate([np.asarray(L1_gnn_gamma).reshape(2, F).T,
                                        np.asarray(L1_gnn_beta).reshape(2, F).T], axis=1)),
    }
    nc = bacc.Bacc("TRN2", target_bir_lowering=False, num_devices=1)
    args = {n: nc.dram_tensor(f"in_{n}", a.shape, mybir.dt.from_np(a.dtype), kind="ExternalInput").ap()
            for n, a in arrays.items()}
    out = nc.dram_tensor("out", (NP, F), mybir.dt.float32, kind="ExternalOutput").ap()
    build_gnn(nc, edges=E, out=out, **args)
    r = run_bass_kernel_spmd(nc, [{f"in_{n}": a for n, a in arrays.items()}], core_ids=[0])
    return r.results[0]["out"][0:N]
```
